# Optimizing a Trainium2 kernel written in Bass

```python
import numpy as np
import jax
import jax.numpy as jnp

def _softmax(x, axis=-1):
    return jax.nn.softmax(x, axis=axis)

def _gelu(x):
    return jax.nn.gelu(x, approximate=True)

def _silu(x):
    return jax.nn.silu(x)

def _sigmoid(x):
    return jax.nn.sigmoid(x)

def _layernorm(x, axis=-1, eps=1e-05):
    m = jnp.mean(x, axis=axis, keepdims=True)
    v = jnp.var(x, axis=axis, keepdims=True)
    return (x - m) / jnp.sqrt(v + eps)

def _scatter_add(tgt, idx, src, axis=0):
    return tgt.at[idx].add(src)

def _segment_sum(src, seg, n):
    return jax.ops.segment_sum(src, seg, n)
kernel_name = 'mk_cond_seq_d1_seqx_r4_7206e9'

def setup_inputs(seed: int=0):
    np.random.seed(seed)
    _w = jnp.asarray

    def _rec_inputs():
        import jax
        import jax.numpy as jnp
        _rk = jax.random.key(seed)
        x = -0.0002928 + 1 * jax.random.normal(jax.random.fold_in(_rk, 1), (16, 256, 256), jnp.float32)
        _lenS = 256 - jax.random.randint(jax.random.fold_in(_rk, 7), (16,), 0, max(1, 256 // 4) + 1, jnp.int32)
        _lenS2 = 256 - jax.random.randint(jax.random.fold_in(_rk, 8), (16,), 0, max(1, 256 // 4) + 1, jnp.int32)
        cond_1024 = 0.000887014 + 1.03683 * jax.random.normal(jax.random.fold_in(_rk, 11), (16, 256), jnp.float32)
        return (x, cond_1024)
    x, cond_1024 = _rec_inputs()

    def _L0_cond_setup():
        import jax, jax.numpy as jnp
        import numpy as np
        B, N, D = (2, 512, 256)
        H, HD = (16, 64)
        E, DD = (8, 1024)
        EPS = 1e-05

        def _ln(x, g, b):
            m = jnp.mean(x, axis=-1, keepdims=True)
            v = jnp.var(x, axis=-1, keepdims=True)
            return (x - m) * jax.lax.rsqrt(v + EPS) * g + b
        key = jax.random.key(seed)
        ks = jax.random.split(key, 16)
        s = 0.02
        return {'x': jax.random.normal(ks[0], (B, N, D), jnp.float32), 't': jax.random.normal(ks[1], (B, 1, D), jnp.float32), 'W_ada': jax.random.normal(ks[2], (D, D), jnp.float32) * s, 'b_ada': jnp.zeros((D,), jnp.float32), 'ln1_g': jnp.ones((D,), jnp.float32), 'ln1_b': jnp.zeros((D,), jnp.float32), 'Wqkv': jax.random.normal(ks[3], (3 * H * HD, D), jnp.float32) * s, 'qn_g': jnp.ones((HD,), jnp.float32), 'qn_b': jnp.zeros((HD,), jnp.float32), 'kn_g': jnp.ones((HD,), jnp.float32), 'kn_b': jnp.zeros((HD,), jnp.float32), 'Wout': jax.random.normal(ks[4], (D, H * HD), jnp.float32) * s, 'mlp_g': jnp.ones((D,), jnp.float32), 'mlp_b': jnp.zeros((D,), jnp.float32), 'Wgate': jax.random.normal(ks[5], (E, D), jnp.float32) * s, 'fc1s': jax.random.normal(ks[6], (E, DD, D), jnp.float32) * s, 'b1s': jnp.zeros((E, DD), jnp.float32), 'fc2s': jax.random.normal(ks[7], (E, D, DD), jnp.float32) * s, 'b2s': jnp.zeros((E, D), jnp.float32)}
    _L0_cond_all = _L0_cond_setup()
    _L0_cond_in = {k: v for k, v in _L0_cond_all.items() if k in ('W_ada', 'b_ada', 'ln1_g', 'ln1_b', 'Wqkv', 'qn_g', 'qn_b', 'kn_g', 'kn_b', 'Wout', 'mlp_g', 'mlp_b', 'Wgate', 'fc1s', 'b1s', 'fc2s', 'b2s')}
    del _L0_cond_all
    return {'x': x, 'cond_1024': cond_1024, 'L0_cond_W_ada': _L0_cond_in['W_ada'], 'L0_cond_b_ada': _L0_cond_in['b_ada'], 'L0_cond_ln1_g': _L0_cond_in['ln1_g'], 'L0_cond_ln1_b': _L0_cond_in['ln1_b'], 'L0_cond_Wqkv': _L0_cond_in['Wqkv'], 'L0_cond_qn_g': _L0_cond_in['qn_g'], 'L0_cond_qn_b': _L0_cond_in['qn_b'], 'L0_cond_kn_g': _L0_cond_in['kn_g'], 'L0_cond_kn_b': _L0_cond_in['kn_b'], 'L0_cond_Wout': _L0_cond_in['Wout'], 'L0_cond_mlp_g': _L0_cond_in['mlp_g'], 'L0_cond_mlp_b': _L0_cond_in['mlp_b'], 'L0_cond_Wgate': _L0_cond_in['Wgate'], 'L0_cond_fc1s': _L0_cond_in['fc1s'], 'L0_cond_b1s': _L0_cond_in['b1s'], 'L0_cond_fc2s': _L0_cond_in['fc2s'], 'L0_cond_b2s': _L0_cond_in['b2s']}

def reference(x, cond_1024, L0_cond_W_ada, L0_cond_b_ada, L0_cond_ln1_g, L0_cond_ln1_b, L0_cond_Wqkv, L0_cond_qn_g, L0_cond_qn_b, L0_cond_kn_g, L0_cond_kn_b, L0_cond_Wout, L0_cond_mlp_g, L0_cond_mlp_b, L0_cond_Wgate, L0_cond_fc1s, L0_cond_b1s, L0_cond_fc2s, L0_cond_b2s):
    import jax
    import jax.numpy as jnp

    def _L0_cond_ref(x, t, W_ada, b_ada, ln1_g, ln1_b, Wqkv, qn_g, qn_b, kn_g, kn_b, Wout, mlp_g, mlp_b, Wgate, fc1s, b1s, fc2s, b2s):
        import jax, jax.numpy as jnp
        import numpy as np
        B, N, D = (2, 512, 256)
        H, HD = (16, 64)
        E, DD = (8, 1024)
        EPS = 1e-05

        def _ln(x, g, b):
            m = jnp.mean(x, axis=-1, keepdims=True)
            v = jnp.var(x, axis=-1, keepdims=True)
            return (x - m) * jax.lax.rsqrt(v + EPS) * g + b
        b, n, d = x.shape
        shift = jax.nn.silu(t) @ W_ada.T + b_ada
        h = _ln(x, ln1_g, ln1_b) + shift
        qkv = (h @ Wqkv.T).reshape(b, n, 3, H, HD)
        q = _ln(qkv[:, :, 0].transpose(0, 2, 1, 3), qn_g, qn_b)
        k = _ln(qkv[:, :, 1].transpose(0, 2, 1, 3), kn_g, kn_b)
        v = qkv[:, :, 2].transpose(0, 2, 1, 3)
        scores = jnp.einsum('bhnd,bhmd->bhnm', q, k) / jnp.sqrt(jnp.float32(HD))
        attn = jax.nn.softmax(scores, axis=-1)
        o = jnp.einsum('bhnm,bhmd->bhnd', attn, v)
        o = o.transpose(0, 2, 1, 3).reshape(b, n, H * HD)
        x = x + o @ Wout.T
        tok = x.reshape(-1, d)
        bs = tok.shape[0]
        gate = jax.nn.softmax(tok @ Wgate.T, axis=-1)
        k_cap = bs // E
        vals, idx = jax.lax.top_k(gate.T, k_cap)
        idx_flat = idx.T.reshape(-1)
        w = vals.T
        g = _ln(tok[idx_flat], mlp_g, mlp_b).reshape(k_cap, E, d)
        y = jnp.einsum('ked,ehd->keh', g, fc1s) + b1s
        y = jax.nn.gelu(y, approximate=True)
        y = jnp.einsum('keh,edh->ked', y, fc2s) + b2s
        y = y * w[..., None]
        tok = tok.at[idx_flat].add(y.reshape(-1, d))
        return tok.reshape(x.shape)
    x = _L0_cond_ref(x, cond_1024[:, None, :], L0_cond_W_ada, L0_cond_b_ada, L0_cond_ln1_g, L0_cond_ln1_b, L0_cond_Wqkv, L0_cond_qn_g, L0_cond_qn_b, L0_cond_kn_g, L0_cond_kn_b, L0_cond_Wout, L0_cond_mlp_g, L0_cond_mlp_b, L0_cond_Wgate, L0_cond_fc1s, L0_cond_b1s, L0_cond_fc2s, L0_cond_b2s)
    return x

_drawn_inputs = setup_inputs


def setup_inputs(seed=0):
    import zlib

    import numpy as np

    out = dict(_drawn_inputs(seed))
    spreads = {'L0_cond_b_ada': (0.0, 0.387),
     'L0_cond_ln1_g': (1.0, 0.6),
     'L0_cond_ln1_b': (0.0, 0.392),
     'L0_cond_qn_g': (1.0, 0.6),
     'L0_cond_qn_b': (0.0, 0.8),
     'L0_cond_kn_g': (1.0, 0.6),
     'L0_cond_kn_b': (0.0, 2.0),
     'L0_cond_mlp_g': (1.0, 0.6),
     'L0_cond_mlp_b': (0.0, 2.0),
     'L0_cond_b1s': (0.0, 0.8),
     'L0_cond_b2s': (0.0, 0.421)}
    factors = {}
    for name, (base, spread) in spreads.items():
        noise = np.random.default_rng([zlib.crc32(name.encode()), seed]).standard_normal(out[name].shape)
        drawn = base * np.exp(spread * noise) if base else spread * noise
        out[name] = jnp.asarray(drawn.astype(out[name].dtype))
    for name, factor in factors.items():
        out[name] = (out[name] * factor).astype(out[name].dtype)
    return out
```

```python
import numpy as np
import concourse.bass as bass
from concourse import mybir
from contextlib import ExitStack

F32 = mybir.dt.float32
F32R = mybir.dt.float32r
BF16 = mybir.dt.bfloat16
I32 = mybir.dt.int32
U32 = mybir.dt.uint32
ALU = mybir.AluOpType
ACT = mybir.ActivationFunctionType
AX = mybir.AxisListType

P = 128
B, N, D = 16, 256, 256
H, HD = 16, 64
E, DD = 8, 1024
TOK = B * N
CAP = TOK // E
EPS = 1e-5
TT = N // P
DC = D // P
HC = DD // P
UNITS = H // 2
GU = UNITS // 2
GW = GU * 2 * HD
TILES = TOK // P
KT = CAP // P
ROW = D + E
BIG = 4096.0
BITS = 30
NEWTON = 3
FIRST_LOOPED, LAST_LOOPED = 2, B - 2


def batch_slots(b):
    cur, nxt, prv = 0 <= b < B, b + 1 < B, 1 <= b <= B
    out = []
    for hp, live in ((0, cur), (4, nxt)):
        if live:
            out += [(hp, 0, "q0", "act"), (hp, 1, "k0", "act"), (hp + 1, 0, "q1", "act"), (hp + 1, 1, "k1", "act"),
                    (hp + 2, 0, "v0", "act"), (hp + 2, 1, "v1", "act")]
    if prv:
        out += [(0, 2, "wout", "dve"), (7, 0, "tokT", "act"), (7, 1, "gate", "dve")]
    if nxt:
        out += [(3, 0, "xT", "act")]
    return sorted(out)


def make_counts():
    table, slots = {}, []
    totals = {}

    def hit(kind, b, key):
        totals[kind] = totals.get(kind, 0) + 1
        table[kind, b, key] = totals[kind]

    for b in range(-1, B + 1):
        cur, nxt, prv = 0 <= b < B, b + 1 < B, 1 <= b <= B
        for hp, pos, name, who in batch_slots(b):
            key = (hp, pos)
            hit("slot", b, key)
            hit(who, b, key)
            slots.append((b, key, who))
            if name[0] in "qk":
                hit("chunk", b, key)
        for hp, live in ((2, True), (6, nxt)):
            if live:
                hit("newton", b, hp)
        for kind, live in (("x_loaded", nxt), ("xr_loaded", cur), ("tok_stored", prv)):
            if live:
                hit(kind, b, 0)
    for n, (b, key, who) in enumerate(slots):
        table["bank", b, key] = n % 2
        table["index", b, key] = n
        if n >= 2:
            pb, pkey, pwho = slots[n - 2]
            table["free", b, key] = (pwho, table[pwho, pb, pkey])
    return table


COUNTS = make_counts()


def through(kind, b, key):
    if isinstance(b, int):
        return COUNTS[kind, b, key]
    first, second = COUNTS[kind, FIRST_LOOPED, key], COUNTS[kind, FIRST_LOOPED + 1, key]
    step = second - first
    assert COUNTS[kind, LAST_LOOPED, key] == first + step * (LAST_LOOPED - FIRST_LOOPED)
    return b * step + (first - step * FIRST_LOOPED)


def bank_free(b, key):
    bi = b if isinstance(b, int) else FIRST_LOOPED + 1
    if ("free", bi, key) not in COUNTS:
        return None
    who, count = COUNTS["free", bi, key]
    if isinstance(b, int):
        return who, count
    who1, c1 = COUNTS["free", bi + 1, key]
    who0, c0 = COUNTS["free", bi - 1, key]
    assert who0 == who1 == who and c1 - count == count - c0
    return who, b * (c1 - count) + (count - (c1 - count) * bi)


def slot_bank(b, key):
    return COUNTS["bank", b if isinstance(b, int) else FIRST_LOOPED, key]


class Need:

    def __init__(self, eng):
        self.eng = eng

    def __call__(self, sem, count):
        if isinstance(count, int) and count <= 0:
            return
        self.eng.wait_ge(sem, count)


def over_batches(eng, batch):
    batch(-1, cur=False, nxt=True, prv=False)
    batch(0, cur=True, nxt=True, prv=False)
    batch(1, cur=True, nxt=True, prv=True)
    with eng.Fori(FIRST_LOOPED, LAST_LOOPED + 1) as b:
        batch(b, cur=True, nxt=True, prv=True)
    batch(B - 1, cur=True, nxt=False, prv=True)
    batch(B, cur=False, nxt=False, prv=True)


def build(nc, x, condT, w_adaT, vecs, w_qkvT, w_outT, w_gateT, experts, b2s, consts, out):
    ctx = ExitStack()
    with ctx:
        place = [ctx]

        def sb(name, shape, dt=F32):
            return place[0].enter_context(nc.sbuf_tensor(name, shape, dt))

        def ps(name, shape):
            return ctx.enter_context(nc.psum_tensor(name, shape, F32))

        def sem(name):
            return ctx.enter_context(nc.semaphore(name))

        rows_dram = nc.dram_tensor("rows_dram", [TOK, ROW], F32, kind="Internal").ap()
        list_dram = nc.dram_tensor("list_dram", [E * CAP], F32, kind="Internal").ap()

        NV = vecs.shape[1]
        NCON = consts.shape[1]
        vec = sb("vec", [P, NV])
        con = sb("con", [P, NCON])
        LN1_G, LN1_B, B_ADA, MLP_G, MLP_B, GQ, BQ, GK, BK = 0, 2, 4, 6, 8, 10, 11, 12, 13
        ident = con[:, 0:P]
        same_expert = con[:, P:2 * P]
        earlier_tile = con[:, 2 * P:3 * P]
        iota32 = con[:, 3 * P:3 * P + 32]
        partno = con[:, 3 * P + 32:3 * P + 33]
        tileno = iota32
        neg_ident = sb("neg_ident", [P, P], BF16)
        same_b = sb("same_b", [P, P], BF16)

        logit = sb("logit", [P, TILES, E])

        scope = ExitStack()
        place[0] = scope
        condT_sb = sb("condT_sb", [P, DC, B])
        sig = sb("sig", [P, DC, B])
        silu = sb("silu", [P, DC, B])
        wada_sb = sb("wada_sb", [P, DC, D])
        bias1 = sb("bias1", [P, DC, B])
        w_hi = sb("w_hi", [P, DC, 3 * H * HD], F32R)
        w_lo = sb("w_lo", [P, DC, 3 * H * HD], F32R)
        wo_sb = sb("wo_sb", [P, UNITS, D])
        wg_sb = sb("wg_sb", [P, DC, E])

        x_sb = sb("x_sb", [P, TT, D])
        xr_sb = sb("xr_sb", [P, TT, D])
        xh = sb("xh", [P, TT, D])
        hT = sb("hT", [P, DC, N])
        hT_hi = sb("hT_hi", [P, DC, N], F32R)
        hT_lo = sb("hT_lo", [P, DC, N], F32R)
        raw = sb("raw", [P, 4, GW])
        sq = [sb(f"sq{i}", [P, GW]) for i in range(2)]
        qn = [sb(f"qn{i}", [P, 4, GW]) for i in range(2)]
        NH = 4 * GU * 2
        ssum = sb("ssum", [P, NH])
        var = sb("var", [P, NH + 4])
        var_half = sb("var_half", [P, NH + 4], I32)
        ny = sb("ny", [P, NH + 4])
        na = sb("na", [P, NH + 4])
        rstd = [sb(f"rstd{i}", [P, NH + 4]) for i in range(2)]
        bn = sb("bn", [P, 4, 6])
        held_v = sb("held_v", [P, 1])
        held_p = sb("held_p", [P, 2])
        mv = sb("mv", [P, 4, 2])
        V = [sb(f"V{i}", [P, TT, GU * 256]) for i in range(2)]
        qz = [sb(f"qz{i}", [P, 2, N]) for i in range(2)]
        kT = [sb(f"kT{i}", [P, N]) for i in range(2)]
        m = [sb(f"m{i}", [P, 4], BF16) for i in range(2)]
        prob = [sb(f"prob{i}", [P, 2 * TT * N]) for i in range(2)]
        rec = sb("rec", [P, N])
        oT = sb("oT", [P, UNITS, N])
        tok = sb("tok", [P, TT, D])
        xh2 = sb("xh2", [P, TT, D])
        tokT = sb("tokT", [P, DC, N])
        scope.close()
        place[0] = ctx

        NP = 2 * P
        top = sb("top", [P, TILES])
        gates = sb("gates", [P, TILES, E])
        gT_ = sb("gates_T", [P, 2, P])
        hit = sb("hit", [P, NP], BF16)
        thr = sb("thr", [P, 1], I32)
        bit = sb("bit", [P, 1], I32)
        trial = sb("trial", [P, 1], I32)
        kept = sb("kept", [P, 1])
        cnt = sb("cnt", [P, 1], BF16)
        above = sb("above", [P, 2, P])
        equal = sb("equal", [P, 2, P])
        n4 = sb("n4", [P, 4])
        d4 = sb("d4", [P, 4])
        first4 = sb("first4", [P, 4])
        zeros = sb("zeros", [P, P])
        rank_a = sb("rank_a", [P, 2, P])
        rank_e = sb("rank_e", [P, 2, P])
        rank = sb("rank", [P, 2, P])
        rank_i = sb("rank_i", [P, TILES * E], I32)
        rank_hi = sb("rank_hi", [P, TILES * E], I32)
        rank_lo = sb("rank_lo", [P, TILES * E], I32)
        RA, RB = 32, 16
        one_a = sb("one_a", [P, TILES * E, RA], BF16)
        one_b = sb("one_b", [P, TILES * E, RB], BF16)
        val_b = sb("val_b", [P, TILES, 2, E // 4, 4 * RB], BF16)
        parts = sb("parts", [P, 2, 2, 4 * RB])
        index_a = sb("index_a", [P, 2, RB])
        lists = sb("lists", [E * KT, P])
        index = sb("index", [P, E * KT], I32)
        FC = DC * DD + HC * D + HC
        fcw = [sb(f"fcw{i}", [P, FC]) for i in range(2)]
        b2_sb = sb("b2_sb", [P, E, D])
        got = [sb(f"got{i}", [P, KT, ROW]) for i in range(2)]
        gT = sb("gT", [P, DC, CAP])
        yT = sb("yT", [P, HC, CAP])
        ysum = sb("ysum", [P, 2, D])
        yout = [sb(f"yout{i}", [P, KT, D]) for i in range(2)]

        pq = ps("pq", [P, 512])
        ch = [ps(f"ch{i}", [P, 512]) for i in range(2)]
        mx = ps("mx", [P, 1024])
        sc = ps("sc", [P, 1024])
        av = ps("av", [P, 512])

        con_in = sem("con_in")
        w_in = sem("w_in")
        wsmall_in = sem("wsmall_in")
        x_in = sem("x_in")
        xr_in = sem("xr_in")
        tok_out = sem("tok_out")
        row_out = sem("row_out")
        consts_ready = sem("consts_ready")
        tanh_done = sem("tanh_done")
        silu_ready = sem("silu_ready")
        shift_done = sem("shift_done")
        bias1_ready = sem("bias1_ready")
        w_ready = sem("w_ready")
        pads_ready = sem("pads_ready")
        qk_transposed = sem("qk_transposed")
        qk_evacuated = sem("qk_evacuated")
        pre_scored = sem("pre_scored")
        max_ready = sem("max_ready")
        scored = sem("scored")
        prob_ready = sem("prob_ready")
        attended = sem("attended")
        normed = sem("normed")
        slot_filled = sem("slot_filled")
        act_read = sem("act_read")
        dve_read = sem("dve_read")
        chunk_summed = sem("chunk_summed")
        rstd_ready = sem("rstd_ready")
        hT_ready = sem("hT_ready")
        hT_split = sem("hT_split")
        qn_ready = sem("qn_ready")
        xh_ready = sem("xh_ready")
        xh2_ready = sem("xh2_ready")
        dve_step = sem("dve_step")
        act_step = sem("act_step")
        pool_step = sem("pool_step")
        free_sem = {"act": act_read, "dve": dve_read}

        class Chain:

            def __init__(self, eng, semaphore, base=0):
                self.eng, self.sem, self.base, self.n = eng, semaphore, base, 0

            def count(self):
                return self.base + self.n

            def base_loop(self, base):
                self.kept, self.base = self.base, self.base + base

            def base_end(self, base):
                self.base = self.kept + base

            def __call__(self, ins):
                self.n += 1
                ins.then_inc(self.sem, 1)
                self.eng.wait_ge(self.sem, self.count())

        logits_ready = sem("logits_ready")
        exp_done = sem("exp_done")
        gates_ready = sem("gates_ready")
        gates_out = sem("gates_out")
        gates_transposed = sem("gates_transposed")
        counted_ready = sem("counted_ready")
        totals_ready = sem("totals_ready")
        n4_ready = sem("n4_ready")
        firsts_ready = sem("firsts_ready")
        rank_ready = sem("rank_ready")
        rank_transposed = sem("rank_transposed")
        hot_ready = sem("hot_ready")
        lists_ready = sem("lists_ready")
        index_a_ready = sem("index_a_ready")
        list_out = sem("list_out")
        list_in = sem("list_in")
        lists_transposed = sem("lists_transposed")
        index_ready = sem("index_ready")
        b2_in = sem("b2_in")
        fc_in = [sem(f"fc_in{i}") for i in range(2)]
        gathered = [sem(f"gathered{i}") for i in range(2)]
        scattered = sem("scattered")
        g_transposed = sem("g_transposed")
        gT_ready = sem("gT_ready")
        fc1_done = sem("fc1_done")
        gelu_done = sem("gelu_done")
        fc2_done = sem("fc2_done")
        fc2_read = sem("fc2_read")
        y_ready = sem("y_ready")

        block = ctx.enter_context(nc.Block())

        def wraw(c, v):
            if v == 0:
                return qn[c][:, :, :].rearrange("p a n -> p (a n)")
            return V[c][:, 0, :]

        def over_experts(eng, expert):
            with eng.Fori(0, E // 2 - 1) as i:
                expert(i * 2, 0, False)
                expert(i * 2 + 1, 1, False)
            expert(E - 2, 0, False)
            expert(E - 1, 1, True)

        def phase23_sync(sp):
            need = Need(sp)
            sp.wait_ge(logits_ready, 1)
            sp.dma_start(b2_sb[:, :, :].rearrange("p e d -> p (e d)"),
                         b2s.rearrange("(o e) d -> o (e d)", o=1).to_broadcast([P, E * D])).then_inc(b2_in, 16)

            def load(e, par):
                src = experts[e] if isinstance(e, int) else experts[bass.ds(e, 1)].rearrange("o p n -> p (o n)")
                sp.dma_start(fcw[par][:, :], src).then_inc(fc_in[par], 16)

            load(0, 0)
            load(1, 1)
            sp.wait_ge(gates_ready, 1)
            sp.dma_start(rows_dram[:, D:ROW].rearrange("(t p) e -> p t e", p=P), gates[:, :, :]).then_inc(gates_out, 16)
            sp.wait_ge(index_a_ready, 1)
            sp.dma_start(list_dram.rearrange("(h q b) -> q h b", h=2, b=RB), index_a[:, :, :]).then_inc(list_out, 16)
            sp.wait_ge(list_out, 16)
            sp.dma_start(lists[:, :], list_dram.rearrange("(m p) -> m p", p=P)).then_inc(list_in, 16)

            def expert(e, par, last):
                need(fc2_done, (e + 1) * KT)
                load(e + 2, par)
            with sp.Fori(0, E // 2 - 1) as i:
                expert(i * 2, 0, False)
                expert(i * 2 + 1, 1, False)

        def phase23_pool(pool):
            pool.wait_ge(index_ready, 1)
            pool.wait_ge(gates_out, 16)
            pool.wait_ge(row_out, B * 16)
            pool.wait_ge(tok_out, B * 16)

            def gather(e):
                par = e % 2
                if e >= 2:
                    pool.wait_ge(y_ready, e - 1)
                for k in range(KT):
                    nc.gpsimd.indirect_dma_start(
                        out=got[par][:, k, :], out_offset=None, in_=rows_dram,
                        in_offset=bass.IndirectOffsetOnAxis(ap=index[:, e * KT + k:e * KT + k + 1].bitcast(U32), axis=0),
                        compute_op=ALU.bypass).then_inc(gathered[par], 16)

            gather(0)
            gather(1)
            for e in range(E):
                pool.wait_ge(y_ready, e + 1)
                if e >= 1:
                    pool.wait_ge(scattered, 16 * KT * e)
                for k in range(KT):
                    nc.gpsimd.indirect_dma_start(
                        out=out.rearrange("b n d -> (b n) d"),
                        out_offset=bass.IndirectOffsetOnAxis(ap=index[:, e * KT + k:e * KT + k + 1].bitcast(U32), axis=0),
                        in_=yout[e % 2][:, k, :], in_offset=None,
                        compute_op=ALU.add).then_inc(scattered, 16)
                if e + 2 < E:
                    gather(e + 2)
            pool.wait_ge(scattered, 16 * KT * E)

        def phase23_scalar(act):
            act.wait_ge(logits_ready, 1)
            nc.scalar.activation(gates[:, :, :], gates[:, :, :], ACT.Exp).then_inc(exp_done, 1)

            def expert(e, par, last):
                act.wait_ge(g_transposed, e + 1)
                for c in range(DC):
                    ins = nc.scalar.activation(gT[:, c, :], mx[:, c * CAP:(c + 1) * CAP], ACT.Identity,
                                               bias=vec[:, MLP_B + c:MLP_B + c + 1], scale=vec[:, MLP_G + c:MLP_G + c + 1])
                ins.then_inc(gT_ready, 1)
                for hc in range(HC):
                    act.wait_ge(fc1_done, e * HC + hc + 1)
                    nc.scalar.activation(yT[:, hc, :], ch[hc % 2][:, :], ACT.Gelu_apprx_tanh,
                                         bias=fcw[par][:, FC - HC + hc:FC - HC + hc + 1]).then_inc(gelu_done, 1)
            over_experts(act, expert)

        def phase23_tensor(pe):
            pe.wait_ge(gates_ready, 1)
            for blk in range(2):
                ins = nc.tensor.transpose(mx[:, blk * P:(blk + 1) * P],
                                          gates[:, blk * 16:(blk + 1) * 16, :].rearrange("p t e -> p (t e)"), ident)
            ins.then_inc(gates_transposed, 1)
            with pe.Fori(0, BITS) as i:
                pe.wait_ge(counted_ready, i + 1)
                nc.tensor.matmul(av[:, 0:1], same_b[:, :], cnt[:, :], start=True, stop=True).then_inc(totals_ready, 1)
            pe.wait_ge(n4_ready, 1)
            nc.tensor.matmul(av[:, 4:8], earlier_tile, n4[:, :], start=True, stop=False)
            nc.tensor.matmul(av[:, 4:8], same_expert, d4[:, :], start=False, stop=True).then_inc(firsts_ready, 1)
            pe.wait_ge(rank_ready, 1)
            for blk in range(2):
                ins = nc.tensor.transpose(mx[:, 512 + blk * P:512 + (blk + 1) * P], rank[:, blk, :], ident)
            ins.then_inc(rank_transposed, 1)
            pe.wait_ge(hot_ready, 1)
            for t in range(TILES):
                for h in range(2):
                    ins = nc.tensor.matmul(ch[h][:, 0:P], one_a[:, t * E + 4 * h:t * E + 4 * h + 4, :].rearrange("p e a -> p (e a)"),
                                           val_b[:, t, :, h, :], start=(t == 0), stop=(t == TILES - 1))
            ins.then_inc(lists_ready, 1)

            pe.wait_ge(list_in, 16)
            nc.tensor.transpose(pq[:, 0:E * KT], lists[:, :], ident[0:E * KT, 0:E * KT]).then_inc(lists_transposed, 1)
            pe.wait_ge(gathered[0], 16 * KT)
            for c in range(DC):
                for k in range(KT):
                    ins = nc.tensor.transpose(mx[:, c * CAP + k * P:c * CAP + (k + 1) * P], got[0][:, k, c * P:(c + 1) * P], ident)
            ins.then_inc(g_transposed, 1)

            def expert(e, par, last, turn):
                w1 = fcw[par][:, 0:DC * DD].rearrange("p (c h) -> p c h", c=DC)
                w2 = fcw[par][:, DC * DD:DC * DD + HC * D].rearrange("p (c d) -> p c d", c=HC)
                pe.wait_ge(fc_in[par], (turn + 1) * 16)
                pe.wait_ge(gT_ready, e + 1)
                for hc in range(HC):
                    if not (isinstance(e, int) and e == 0 and hc < 2):
                        if hc < 2 and par == 0:
                            pe.wait_ge(gelu_done, e * HC)
                        else:
                            pe.wait_ge(gelu_done, e * HC + hc - 1)
                    for c in range(DC):
                        ins = nc.tensor.matmul(ch[hc % 2][:, :], w1[:, c, hc * P:(hc + 1) * P], gT[:, c, :], start=(c == 0), stop=(c == DC - 1))
                    ins.then_inc(fc1_done, 1)
                if not last:
                    pe.wait_ge(gathered[1 - par], (turn + 1 + par) * (16 * KT))
                    for c in range(DC):
                        for k in range(KT):
                            ins = nc.tensor.transpose(mx[:, c * CAP + k * P:c * CAP + (k + 1) * P], got[1 - par][:, k, c * P:(c + 1) * P], ident)
                    ins.then_inc(g_transposed, 1)
                pe.wait_ge(gelu_done, (e + 1) * HC)
                for k in range(KT):
                    bank = (av, pq)[k % 2]
                    if k < 2:
                        if not (isinstance(e, int) and e == 0):
                            pe.wait_ge(fc2_read, e * KT + k - 1)
                    else:
                        pe.wait_ge(fc2_read, e * KT + k - 1)
                    for hc in range(HC):
                        ins = nc.tensor.matmul(bank[:, 0:D], yT[:, hc, k * P:(k + 1) * P], w2[:, hc, :], start=(hc == 0), stop=(hc == HC - 1))
                    ins.then_inc(fc2_done, 1)

            expert(0, 0, False, 0)
            expert(1, 1, False, 0)
            with pe.Fori(1, E // 2 - 1) as i:
                expert(i * 2, 0, False, i)
                expert(i * 2 + 1, 1, False, i)
            expert(E - 2, 0, False, E // 2 - 1)
            expert(E - 1, 1, True, E // 2 - 1)

        def phase23_vector(dve, chain):
            need = Need(dve)
            V_ = nc.vector
            dve.wait_ge(dve_read, 2 * B)
            chain(V_.tensor_reduce(top[:, :], logit[:, :, :], AX.X, ALU.max))
            top3 = top[:, :].rearrange("p (t o) -> p t o", o=1).to_broadcast([P, TILES, E])
            V_.tensor_tensor(gates[:, :, :], logit[:, :, :], top3, ALU.subtract).then_inc(logits_ready, 1)
            dve.wait_ge(exp_done, 1)
            chain(V_.tensor_reduce(top[:, :], gates[:, :, :], AX.X, ALU.add))
            chain(V_.reciprocal(top[:, :], top[:, :]))
            V_.tensor_tensor(gates[:, :, :], gates[:, :, :], top3, ALU.mult).then_inc(gates_ready, 1)
            V_.memset(zeros[:, :], 0.0)
            V_.memset(d4[:, :], 0.0)
            V_.memset(bit[:, :], 1 << (BITS - 1))
            chain(V_.memset(thr[:, :], 0))
            dve.wait_ge(gates_transposed, 1)
            chain(V_.tensor_copy(gT_[:, :, :].rearrange("p b t -> p (b t)"), mx[:, 0:NP]))
            before = chain.n
            with dve.Fori(0, BITS) as i:
                chain.base_loop(i * 4)
                chain(V_.tensor_tensor(trial[:, :], thr[:, :], bit[:, :], ALU.bitwise_or))
                V_.tensor_scalar(hit[:, :], gT_[:, :, :].rearrange("p b t -> p (b t)"), trial[:, :].bitcast(F32), 0.0,
                                 ALU.is_ge, ALU.add, accum_out=cnt[:, :]).then_inc(counted_ready, 1)
                chain(V_.tensor_scalar(bit[:, :], bit[:, :], 1, None, ALU.logical_shift_right))
                dve.wait_ge(totals_ready, i + 1)
                chain(V_.scalar_tensor_tensor(kept[:, :], av[:, 0:1], CAP - 0.5, trial[:, :].bitcast(F32), ALU.is_ge, ALU.mult))
                chain(V_.tensor_tensor(thr[:, :].bitcast(F32), thr[:, :].bitcast(F32), kept[:, :], ALU.max))
            assert chain.n - before == 4
            chain.base_end(4 * (BITS - 1))
            t_ = thr[:, :].bitcast(F32)
            V_.tensor_scalar(above[:, :, :], gT_[:, :, :], t_, None, ALU.is_gt)
            chain(V_.tensor_scalar(equal[:, :, :], gT_[:, :, :], t_, None, ALU.is_equal))
            V_.tensor_reduce(n4[:, 0:2], above[:, :, :], AX.X, ALU.add)
            chain(V_.tensor_reduce(n4[:, 2:4], equal[:, :, :], AX.X, ALU.add))
            for i in range(3):
                ins = V_.tensor_tensor(d4[:, i + 1:i + 2], d4[:, i:i + 1], n4[:, i:i + 1], ALU.add)
                if i < 2:
                    chain(ins)
            ins.then_inc(n4_ready, 1)
            dve.wait_ge(firsts_ready, 1)
            chain(V_.tensor_scalar(first4[:, :], av[:, 4:8], -1.0, None, ALU.add))
            for blk in range(2):
                V_.tensor_tensor_scan(rank_a[:, blk, :], above[:, blk, :], zeros[:, :], first4[:, blk:blk + 1], ALU.add, ALU.add)
                ins = V_.tensor_tensor_scan(rank_e[:, blk, :], equal[:, blk, :], zeros[:, :], first4[:, 2 + blk:3 + blk], ALU.add, ALU.add)
            chain(ins)
            V_.tensor_tensor(rank_a[:, :, :], rank_a[:, :, :], above[:, :, :], ALU.mult)
            chain(V_.tensor_tensor(rank_e[:, :, :], rank_e[:, :, :], equal[:, :, :], ALU.mult))
            V_.tensor_tensor(rank_a[:, :, :], rank_a[:, :, :], rank_e[:, :, :], ALU.add)
            chain(V_.tensor_tensor(above[:, :, :], above[:, :, :], equal[:, :, :], ALU.add))
            chain(V_.tensor_scalar(above[:, :, :], above[:, :, :], -BIG, BIG, ALU.mult, ALU.add))
            V_.tensor_tensor(rank[:, :, :], rank_a[:, :, :], above[:, :, :], ALU.add).then_inc(rank_ready, 1)
            dve.wait_ge(rank_transposed, 1)
            chain(V_.tensor_copy(rank_i[:, :], mx[:, 512:512 + NP]))
            V_.tensor_scalar(rank_hi[:, :], rank_i[:, :], 4, None, ALU.logical_shift_right)
            chain(V_.tensor_scalar(rank_lo[:, :], rank_i[:, :], RB - 1, None, ALU.bitwise_and))
            TE = TILES * E

            def spread(ap, k):
                return ap.rearrange("p (n o) -> p n o", o=1).to_broadcast([P, TE, k])

            def ramp(k):
                return iota32[:, 0:k].rearrange("p (o k) -> p o k", o=1).to_broadcast([P, TE, k])
            V_.tensor_tensor(one_b[:, :, :], spread(rank_lo[:, :], RB), ramp(RB), ALU.is_equal)
            chain(V_.tensor_tensor(one_a[:, :, :], spread(rank_hi[:, :], RA), ramp(RA), ALU.is_equal))
            hot = one_b[:, :, :].rearrange("p (t h e) b -> p t h (e b)", t=TILES, h=2)
            V_.tensor_scalar(val_b[:, :, 0, :, :], hot, partno, None, ALU.mult)
            V_.tensor_tensor(val_b[:, :, 1, :, :].rearrange("p t h c -> p t (h c)") if False else val_b[:, :, 1, :, :], hot,
                             tileno.rearrange("p (t o q) -> p t o q", o=1, q=1).to_broadcast([P, TILES, 2, 4 * RB]), ALU.mult).then_inc(hot_ready, 1)
            dve.wait_ge(lists_ready, 1)
            for h in range(2):
                ins = V_.tensor_copy(parts[:, h, :, :].rearrange("p v c -> p (v c)"), ch[h][:, 0:P])
            chain(ins)
            for h in range(2):
                for e in range(4):
                    q = slice(32 * e, 32 * e + 32)
                    ins = V_.scalar_tensor_tensor(index_a[q, h, :], parts[q, h, 1, e * RB:(e + 1) * RB], float(P),
                                                  parts[q, h, 0, e * RB:(e + 1) * RB], ALU.mult, ALU.add)
            ins.then_inc(index_a_ready, 1)
            dve.wait_ge(lists_transposed, 1)
            V_.tensor_copy(index[:, :], pq[:, 0:E * KT]).then_inc(index_ready, 1)

            dve.wait_ge(b2_in, 16)

            def expert(e, par, last):
                for k in range(KT):
                    dve.wait_ge(fc2_done, e * KT + k + 1)
                    if k == 0 and not (isinstance(e, int) and e < 2):
                        dve.wait_ge(scattered, (e - 1) * (16 * KT))
                    b2 = (b2_sb[:, e, :] if isinstance(e, int) else
                          b2_sb[:, :, :].rearrange("p e d -> p (e d)")[:, bass.ds(e * D, D)])
                    w = (got[par][:, k, D + e:D + e + 1] if isinstance(e, int) else got[par][:, k, bass.ds(e + D, 1)])
                    ins = V_.tensor_tensor(ysum[:, k % 2, :], (av, pq)[k % 2][:, 0:D], b2, ALU.add)
                    ins.then_inc(fc2_read, 1)
                    dve.wait_ge(fc2_read, e * KT + k + 1)
                    ins = V_.tensor_scalar(yout[par][:, k, :], ysum[:, k % 2, :], w, None, ALU.mult)
                ins.then_inc(y_ready, 1)
            expert(0, 0, False)
            expert(1, 1, False)
            with dve.Fori(1, E // 2) as i:
                expert(i * 2, 0, False)
                expert(i * 2 + 1, 1, False)

        def sync_batch(sp):
            need = Need(sp)

            def batch(b, cur, nxt, prv):
                if nxt:
                    need(xh_ready, b + 1)
                    sp.dma_start(x_sb[:, :, :], x[bass.ds(b + 1, 1)].rearrange("o (t p) d -> p (o t) d", p=P)
                                 if not isinstance(b, int) else x[b + 1].rearrange("(t p) d -> p t d", p=P)).then_inc(x_in, 16)
                if prv:
                    need(dve_read, through("dve", b, (0, 2)))
                    dst = (out[bass.ds(b - 1, 1)].rearrange("o (t p) d -> p (o t) d", p=P)
                           if not isinstance(b, int) else out[b - 1].rearrange("(t p) d -> p t d", p=P))
                    sp.dma_start(dst, tok[:, :, :]).then_inc(tok_out, 16)
                if cur:
                    src = (x[bass.ds(b, 1)].rearrange("o (t p) d -> p (o t) d", p=P)
                           if not isinstance(b, int) else x[b].rearrange("(t p) d -> p t d", p=P))
                    sp.dma_start(xr_sb[:, :, :], src).then_inc(xr_in, 16)
                if prv:
                    need(xh2_ready, b)
                    r = (rows_dram[bass.ds((b - 1) * N, N)] if not isinstance(b, int)
                         else rows_dram[(b - 1) * N:b * N])
                    sp.dma_start(r[:, 0:D].rearrange("(t p) d -> p t d", p=P), xh2[:, :, :]).then_inc(row_out, 16)
            return batch

        @block.sync
        def _(sp):
            sp.dma_start(con[:, :], consts).then_inc(con_in, 16)
            sp.dma_start(vec[:, :], vecs).then_inc(con_in, 16)
            sp.dma_start(condT_sb[:, :, :], condT).then_inc(con_in, 16)
            sp.dma_start(wada_sb[:, :, :], w_adaT).then_inc(con_in, 16)
            for c in range(DC):
                sp.dma_start(wraw(c, 0), w_qkvT[:, c, 0:2048]).then_inc(w_in, 16)
                sp.dma_start(wraw(c, 1), w_qkvT[:, c, 2048:3072]).then_inc(w_in, 16)
            sp.dma_start(wo_sb[:, :, :], w_outT).then_inc(wsmall_in, 16)
            sp.dma_start(wg_sb[:, :, :], w_gateT).then_inc(wsmall_in, 16)
            over_batches(sp, sync_batch(sp))
            phase23_sync(sp)

        @block.gpsimd
        def _(pool):
            need = Need(pool)
            for i in range(2):
                nc.gpsimd.memset(qz[i][:, :, :], 0.0).then_inc(pads_ready, 1)
            pool.wait_ge(w_ready, 1)
            for i in range(2):
                for jt in range(TT):
                    ones = V[i][:, jt, :].rearrange("p (u c) -> p u c", c=256)[:, :, HD:HD + 128]
                    nc.gpsimd.memset(ones, 1.0).then_inc(pads_ready, 1)

            def batch(b, cur, nxt, prv):
                def normalise(g, hp):
                    par = 0 if hp == 6 else 1
                    need(rstd_ready, through("newton", b, hp))
                    need(qk_transposed, (g - 1) * GU)
                    for c in range(4):
                        src = raw[:, c, :].rearrange("p (h d) -> p h d", d=HD)
                        r = rstd[par][:, c * 8:(c + 1) * 8].rearrange("p (h o) -> p h o", o=1).to_broadcast([P, 8, HD])
                        last = nc.gpsimd.tensor_tensor(qn[par][:, c, :].rearrange("p (h d) -> p h d", d=HD), src, r, ALU.mult)
                    last.then_inc(qn_ready, 1)

                if cur:
                    normalise(b * 2 + 1, 2)
                if nxt:
                    need(rstd_ready, through("newton", b, 2))
                    if cur:
                        need(slot_filled, through("slot", b, (0, 0)))
                    nc.gpsimd.tensor_tensor(held_p[:, 0:1], rstd[1][:, NH:NH + 1], rstd[1][:, NH:NH + 1], ALU.add)
                    for t in range(TT):
                        last = nc.gpsimd.tensor_scalar(xh[:, t, :], x_sb[:, t, :], mv[:, t, 0:1],
                                                       rstd[1][:, NH + t:NH + t + 1], ALU.subtract, ALU.mult)
                    last.then_inc(xh_ready, 1)
                if prv:
                    need(rstd_ready, through("newton", b, 2))
                    need(row_out, (b - 1) * 16)
                    nc.gpsimd.tensor_tensor(held_p[:, 1:2], rstd[1][:, NH:NH + 1], rstd[1][:, NH:NH + 1], ALU.add)
                    for t in range(TT):
                        last = nc.gpsimd.tensor_scalar(xh2[:, t, :], tok[:, t, :], mv[:, 2 + t, 0:1],
                                                       rstd[1][:, NH + 2 + t:NH + 3 + t], ALU.subtract, ALU.mult)
                    last.then_inc(xh2_ready, 1)
                if nxt:
                    normalise(b * 2 + 2, 6)

            over_batches(pool, batch)
            phase23_pool(pool)

        @block.scalar
        def _(act):
            need = Need(act)
            act.wait_ge(con_in, 64)
            nc.scalar.activation(sig[:, :, :], condT_sb[:, :, :], ACT.Tanh, scale=0.5).then_inc(tanh_done, 1)

            def slot(b, hp, pos, g=None):
                key = (hp, pos)
                bank = ch[slot_bank(b, key)]
                name = {(0, 0): "q", (0, 1): "k", (1, 0): "q", (1, 1): "k", (2, 0): "v", (2, 1): "v"}.get((hp % 4, pos))
                need(slot_filled, through("slot", b, key))
                if name in ("q", "k"):
                    c = (hp % 4) * 2 + pos
                    need(qn_ready, g)
                    nc.scalar.activation(raw[:, c, :], bank[:, :], ACT.Copy)
                    need(chunk_summed, through("chunk", b, key) - 2)
                    nc.scalar.activation(sq[c % 2][:, :], bank[:, :], ACT.Square).then_inc(act_read, 1)
                else:
                    need(attended, (g - 1) * GU)
                    par = 0 if hp >= 4 else 1
                    dst = V[par][:, pos, :].rearrange("p (u a c) -> p u a c", u=GU, a=4)
                    src = bank[:, :].rearrange("p (u a c) -> p u a c", u=GU, a=2)
                    nc.scalar.activation(dst[:, :, 0:4:3, :], src, ACT.Copy).then_inc(act_read, 1)

            def batch(b, cur, nxt, prv):
                for hp in range(UNITS):
                    u = b * UNITS + hp
                    par = (hp + 1) % 2
                    if (cur and nxt) or (cur and hp < UNITS - 1) or (nxt and hp == UNITS - 1):
                        need(qk_transposed, u + 2)
                        need(scored, u)
                        if isinstance(b, int) and b < 0:
                            need(pads_ready, 2)
                        nc.scalar.activation(qz[par][0:64, 0, :], pq[0:64, 0:N], ACT.Identity,
                                             bias=vec[0:64, BQ:BQ + 1], scale=vec[0:64, GQ:GQ + 1])
                        nc.scalar.activation(qz[par][64:128, 1, :], pq[64:128, 0:N], ACT.Identity,
                                             bias=vec[64:128, BQ:BQ + 1], scale=vec[64:128, GQ:GQ + 1])
                        nc.scalar.activation(kT[par][:, :], pq[:, N:2 * N], ACT.Identity,
                                             bias=vec[:, BK:BK + 1], scale=vec[:, GK:GK + 1]).then_inc(qk_evacuated, 1)
                    live = cur if hp < 4 else nxt
                    g = b * 2 + (1 if hp < 4 else 2)
                    if hp % 4 < 3 and live:
                        slot(b, hp, 0, g)
                    if hp == 3 and nxt:
                        need(slot_filled, through("slot", b, (3, 0)))
                        need(bias1_ready, 1)
                        need(hT_split, b + 1)
                        bank = ch[slot_bank(b, (3, 0))]
                        for c in range(DC):
                            bias = (bias1[:, c, b + 1:b + 2] if isinstance(b, int) else bias1[:, c, bass.ds(b + 1, 1)])
                            ins = nc.scalar.activation(hT[:, c, :], bank[:, c * N:(c + 1) * N], ACT.Identity,
                                                       bias=bias, scale=vec[:, LN1_G + c:LN1_G + c + 1])
                        ins.then_inc(act_read, 1)
                    if hp == 7 and prv:
                        need(slot_filled, through("slot", b, (7, 0)))
                        nc.scalar.activation(tokT[:, :, :].rearrange("p c n -> p (c n)"),
                                             ch[slot_bank(b, (7, 0))][:, :], ACT.Copy).then_inc(act_read, 1)
                    if cur:
                        need(scored, u + 1)
                        need(attended, u - 1)
                        nc.scalar.activation(prob[hp % 2][:, :], sc[:, :], ACT.Exp, scale=HD ** -0.5).then_inc(prob_ready, 1)
                    if hp % 4 < 3 and live:
                        slot(b, hp, 1, g)

            over_batches(act, batch)
            phase23_scalar(act)

        def rsqrt(chain, n, dst):
            v, y, a = var[:, 0:n], ny[:, 0:n], na[:, 0:n]
            half = var_half[:, 0:n]
            chain(nc.vector.tensor_scalar(half, v.bitcast(I32), 1, None, ALU.logical_shift_right))
            chain(nc.vector.tensor_scalar(y.bitcast(I32), half, -1.0, float(0x5F3759DF), ALU.mult, ALU.add))
            for r in range(NEWTON):
                chain(nc.vector.scalar_tensor_tensor(a, y, -0.5, y, ALU.mult, ALU.mult))
                chain(nc.vector.tensor_tensor(a, a, v, ALU.mult))
                if r < NEWTON - 1:
                    chain(nc.vector.scalar_tensor_tensor(y, a, 1.5, y, ALU.add, ALU.mult))
                else:
                    nc.vector.scalar_tensor_tensor(dst[:, 0:n], a, 1.5, y, ALU.add, ALU.mult).then_inc(rstd_ready, 1)

        @block.vector
        def _(dve):
            need = Need(dve)
            chain = Chain(dve, dve_step)
            dve.wait_ge(con_in, 64)
            nc.vector.tensor_scalar(neg_ident[:, :], ident, -1.0, None, ALU.mult).then_inc(consts_ready, 1)
            nc.vector.tensor_copy(same_b[:, :], same_expert).then_inc(consts_ready, 1)
            nc.vector.memset(mv[:, :, :], 1.0)
            chain(nc.vector.memset(var[:, :], 1.0))
            dve.wait_ge(tanh_done, 1)
            chain(nc.vector.scalar_tensor_tensor(sig[:, :, :], sig[:, :, :], 1.0, condT_sb[:, :, :], ALU.add, ALU.mult))
            nc.vector.tensor_scalar(silu[:, :, :], sig[:, :, :], 0.5, None, ALU.mult).then_inc(silu_ready, 1)
            dve.wait_ge(shift_done, 1)
            for c in range(DC):
                ins = nc.vector.tensor_scalar(bias1[:, c, :], av[:, c * B:(c + 1) * B], vec[:, B_ADA + c:B_ADA + c + 1],
                                              vec[:, LN1_B + c:LN1_B + c + 1], ALU.add, ALU.add)
            ins.then_inc(bias1_ready, 1)
            dve.wait_ge(w_in, 2 * DC * 16)
            for c in range(DC):
                wqk = wraw(c, 0)
                means = raw[:, c, 0:2 * H]
                w3 = wqk.rearrange("p (h d) -> p h d", d=HD)
                chain(nc.vector.tensor_reduce(means, w3, AX.X, ALU.add))
                chain(nc.vector.tensor_scalar(means, means, 1.0 / HD, None, ALU.mult))
                chain(nc.vector.tensor_tensor(w3, w3, means.rearrange("p (h o) -> p h o", o=1).to_broadcast([P, 2 * H, HD]), ALU.subtract))
                for a, bb, src in ((0, 2048, wqk), (2048, 3072, wraw(c, 1))):
                    chain(nc.vector.tensor_copy(w_hi[:, c, a:bb], src))
                    ins = nc.vector.tensor_tensor(w_lo[:, c, a:bb], src, w_hi[:, c, a:bb].bitcast(F32), ALU.subtract)
            ins.then_inc(w_ready, 1)

            def row_stats(rows, at):
                for t in range(TT):
                    ins = nc.vector.bn_stats(bn[:, at + t, :], rows[:, t, :])
                ins.then_inc(dve_step, 1)
                chain.n += 1
                dve.wait_ge(dve_step, chain.count())
                nc.vector.memset(held_v[:, :], 0.0)
                for t in range(TT):
                    ins = nc.vector.bn_aggr(mv[:, at + t, :], bn[:, at + t, :])
                chain(ins)

            def head_sums(b, hp, pos):
                c = (hp % 4) * 2 + pos
                need(act_read, through("act", b, (hp, pos)))
                nc.vector.tensor_reduce(ssum[:, c * 8:(c + 1) * 8],
                                        sq[c % 2][:, :].rearrange("p (h d) -> p h d", d=HD), AX.X, ALU.add).then_inc(chunk_summed, 1)

            def batch(b, cur, nxt, prv):
                for hp in range(UNITS):
                    u = b * UNITS + hp
                    live = cur if hp < 4 else nxt
                    if hp in (2, 6) and (hp == 2 or nxt):
                        if live:
                            need(chunk_summed, through("chunk", b, (hp - 1, 1)))
                            chain(nc.vector.tensor_scalar(var[:, 0:NH], ssum[:, :], 1.0 / HD, EPS, ALU.mult, ALU.add))
                        if hp == 2:
                            chain(nc.vector.tensor_scalar(var[:, NH:NH + 4], mv[:, :, 1], EPS, None, ALU.add))
                            if cur:
                                need(xh_ready, b + 1)
                                need(qn_ready, b * 2)
                            if prv:
                                need(xh2_ready, b - 1)
                        else:
                            need(qn_ready, b * 2 + 1)
                        rsqrt(chain, NH + 4 if hp == 2 else NH, rstd[1 if hp == 2 else 0])
                    if (cur and hp > 0) or (hp == 0 and prv):
                        need(attended, u)
                        pair = (hp - 1) % UNITS
                        if hp == 1 and prv:
                            need(slot_filled, through("slot", b, (0, 2)))
                        need(normed, u - 1)
                        nc.vector.reciprocal(rec[0:64, :], av[64:128, 0:N])
                        chain(nc.vector.reciprocal(rec[64:128, :], av[0:64, N:2 * N]))
                        nc.vector.tensor_tensor(oT[0:64, pair, :], av[0:64, 0:N], rec[0:64, :], ALU.mult)
                        nc.vector.tensor_tensor(oT[64:128, pair, :], av[64:128, N:2 * N], rec[64:128, :], ALU.mult).then_inc(normed, 1)
                    if hp == 1 and prv:
                        need(dve_read, through("dve", b, (0, 2)))
                        row_stats(tok, 2)
                    if hp == 1 and nxt:
                        need(x_in, (b + 2) * 16)
                        row_stats(x_sb, 0)
                    if hp % 4 < 2 and live:
                        head_sums(b, hp, 0)
                        head_sums(b, hp, 1)
                    if hp == 3 and nxt:
                        need(act_read, through("act", b, (3, 0)))
                        chain(nc.vector.tensor_copy(hT_hi[:, :, :], hT[:, :, :]))
                        nc.vector.tensor_tensor(hT_lo[:, :, :], hT[:, :, :], hT_hi[:, :, :].bitcast(F32), ALU.subtract).then_inc(hT_split, 1)
                    if hp == 0 and prv:
                        need(slot_filled, through("slot", b, (0, 2)))
                        need(xr_in, b * 16)
                        need(tok_out, (b - 1) * 16)
                        need(xh2_ready, b - 1)
                        nc.vector.tensor_tensor(tok[:, :, :].rearrange("p t d -> p (t d)"), ch[slot_bank(b, (0, 2))][:, :],
                                                xr_sb[:, :, :].rearrange("p t d -> p (t d)"), ALU.add).then_inc(dve_read, 1)
                    if hp == 7 and prv:
                        need(slot_filled, through("slot", b, (7, 1)))
                        dst = (logit[:, (b - 1) * TT:b * TT, :].rearrange("p t e -> p (t e)") if isinstance(b, int)
                               else logit[:, :, :].rearrange("p t e -> p (t e)")[:, bass.ds((b - 1) * TT * E, TT * E)])
                        nc.vector.tensor_copy(dst, ch[slot_bank(b, (7, 1))][:, 0:TT * E]).then_inc(dve_read, 1)
                    if (cur and nxt) or (cur and hp < UNITS - 1) or (nxt and hp == UNITS - 1):
                        need(pre_scored, u + 2)
                        need(scored, u)
                        nc.vector.tensor_reduce(m[(hp + 1) % 2][:, :], mx[:, :].rearrange("p (a j) -> p a j", a=4),
                                                AX.X, ALU.max).then_inc(max_ready, 1)


            per = 36
            def counted(b, cur, nxt, prv):
                before = chain.n
                if not isinstance(b, int):
                    chain.base = (b - FIRST_LOOPED) * per
                batch(b, cur, nxt, prv)
                if not isinstance(b, int):
                    assert chain.n - before == per, chain.n - before
                    chain.base = per * (LAST_LOOPED - FIRST_LOOPED)
            over_batches(dve, counted)
            phase23_vector(dve, chain)

        def three_passes(psum, l_hi, l_lo, r_hi, r_lo, first, last):
            nc.tensor.matmul(psum, l_lo, r_hi, start=first, stop=False)
            nc.tensor.matmul(psum, l_hi, r_lo, start=False, stop=False)
            return nc.tensor.matmul(psum, l_hi, r_hi, start=False, stop=last)

        @block.tensor
        def _(pe):
            need = Need(pe)
            pe.wait_ge(con_in, 64)
            pe.wait_ge(silu_ready, 1)
            for mc in range(DC):
                for c in range(DC):
                    ins = nc.tensor.matmul(av[:, mc * B:(mc + 1) * B], wada_sb[:, c, mc * P:(mc + 1) * P], silu[:, c, :],
                                           start=(c == 0), stop=(c == DC - 1))
            ins.then_inc(shift_done, 1)
            pe.wait_ge(consts_ready, 2)

            def take_bank(b, key):
                free = bank_free(b, key)
                if free:
                    need(free_sem[free[0]], free[1])
                return ch[slot_bank(b, key)]

            def slot(b, hp, pos):
                bank = take_bank(b, (hp, pos))
                half = 1 if hp < 4 else 0
                if hp % 4 == 0 and pos == 0:
                    need(hT_split, b + 1 if hp < 4 else b + 2)
                if isinstance(b, int) and b < 0 and hp == 4 and pos == 0:
                    need(w_ready, 1)
                if hp % 4 < 2:
                    t, col = hp % 4, pos * H * HD + half * GW
                else:
                    t, col = pos, 2 * H * HD + half * GW
                for c in range(DC):
                    ins = three_passes(bank[:, :], hT_hi[:, c, t * P:(t + 1) * P], hT_lo[:, c, t * P:(t + 1) * P],
                                       w_hi[:, c, col:col + GW], w_lo[:, c, col:col + GW], c == 0, c == DC - 1)
                ins.then_inc(slot_filled, 1)

            def batch(b, cur, nxt, prv):
                for hp in range(UNITS):
                    u = b * UNITS + hp
                    ahead = (cur and nxt) or (cur and hp < UNITS - 1) or (nxt and hp == UNITS - 1)
                    npar = (hp + 1) % 2
                    live = cur if hp < 4 else nxt
                    if ahead:
                        gpar, i = ((hp + 1) // GU) % 2, (hp + 1) % GU
                        need(qn_ready, b * 2 + (hp + 1) // GU + 1)
                        need(qk_evacuated, u + 1)
                        for c, at in ((0, 0), (2, 1), (1, 2), (3, 3)):
                            ins = nc.tensor.transpose(pq[:, at * P:(at + 1) * P], qn[gpar][:, c, i * P:(i + 1) * P], ident)
                        ins.then_inc(qk_transposed, 1)
                    if hp % 4 < 3 and live:
                        slot(b, hp, 0)
                    if hp == 3 and nxt:
                        bank = take_bank(b, (3, 0))
                        need(xh_ready, b + 2)
                        for c in range(DC):
                            for t in range(TT):
                                ins = nc.tensor.transpose(bank[:, c * N + t * P:c * N + (t + 1) * P], xh[:, t, c * P:(c + 1) * P], ident)
                        ins.then_inc(slot_filled, 1)
                    if hp == 7 and prv:
                        bank = take_bank(b, (7, 0))
                        need(dve_read, through("dve", b, (0, 2)))
                        for c in range(DC):
                            for t in range(TT):
                                ins = nc.tensor.transpose(bank[:, c * N + t * P:c * N + (t + 1) * P], tok[:, t, c * P:(c + 1) * P], ident)
                        ins.then_inc(slot_filled, 1)
                    if (cur and hp > 0) or (hp == 0 and prv):
                        need(prob_ready, u)
                        need(normed, u - 1)
                        i = (hp - 1) % GU
                        gpar = ((hp - 1) // GU) % 2
                        if i == 0:
                            need(act_read, through("act", b, (2, 1)) if hp == 5 else through("act", b, (0, 0)) - 1)
                            if isinstance(b, int) and b == 0:
                                need(pads_ready, 6)
                        for hh in range(2):
                            for jt in range(TT):
                                ins = nc.tensor.matmul(av[:, hh * N:(hh + 1) * N], V[gpar][:, jt, i * 256 + hh * P:i * 256 + (hh + 1) * P],
                                                       prob[(hp - 1) % 2][:, hh * TT * N + jt * N:hh * TT * N + (jt + 1) * N],
                                                       start=(jt == 0), stop=(jt == TT - 1))
                        ins.then_inc(attended, 1)
                    if cur:
                        need(prob_ready, u)
                        need(max_ready, u + 1)
                        par = hp % 2
                        for hh in range(2):
                            for jt in range(TT):
                                at = hh * TT * N + jt * N
                                nc.tensor.matmul(sc[:, at:at + N], kT[par][:, jt * P:(jt + 1) * P], qz[par][:, hh, :], start=True, stop=False)
                                for it in range(TT):
                                    ins = nc.tensor.matmul(sc[:, at + it * P:at + (it + 1) * P],
                                                           m[par][:, it * 2 + hh:it * 2 + hh + 1].to_broadcast([P, P]),
                                                           neg_ident[:, :], start=False, stop=(it == TT - 1))
                        ins.then_inc(scored, 1)
                    if hp % 4 < 3 and live:
                        slot(b, hp, 1)
                    if hp == 0 and prv:
                        bank = take_bank(b, (0, 2))
                        need(normed, u)
                        if isinstance(b, int) and b == 1:
                            need(wsmall_in, 32)
                        for t in range(TT):
                            for pair in range(UNITS):
                                ins = nc.tensor.matmul(bank[:, t * D:(t + 1) * D], oT[:, pair, t * P:(t + 1) * P], wo_sb[:, pair, :],
                                                       start=(pair == 0), stop=(pair == UNITS - 1))
                        ins.then_inc(slot_filled, 1)
                    if hp == 7 and prv:
                        bank = take_bank(b, (7, 1))
                        need(act_read, through("act", b, (7, 0)))
                        for t in range(TT):
                            for c in range(DC):
                                ins = nc.tensor.matmul(bank[:, t * E:(t + 1) * E], tokT[:, c, t * P:(t + 1) * P], wg_sb[:, c, :],
                                                       start=(c == 0), stop=(c == DC - 1))
                        ins.then_inc(slot_filled, 1)
                    if ahead:
                        need(qk_evacuated, u + 2)
                        need(max_ready, u + 1)
                        qb = qz[npar][:, :, :].bitcast(BF16)
                        kb = kT[npar][:, :].bitcast(BF16)
                        for it in range(TT):
                            for hh in range(2):
                                at = (it * 2 + hh) * N
                                ins = nc.tensor.matmul(mx[:, at:at + N], qb[:, hh, 2 * it * P + 1:2 * (it + 1) * P:2], kb[:, 1:2 * N:2],
                                                       start=True, stop=True)
                        ins.then_inc(pre_scored, 1)

            over_batches(pe, batch)
            phase23_tensor(pe)


def kernel(**inputs):
    import concourse.bacc as bacc
    from concourse.bass_utils import run_bass_kernel_spmd

    a = {k.removeprefix("L0_cond_"): np.asarray(v) for k, v in inputs.items()}

    def by_partition(w):
        return np.ascontiguousarray(w.reshape(-1, P, w.shape[-1]).transpose(1, 0, 2))

    def columns(v):
        return v.reshape(-1, P).T

    twice = lambda v: np.concatenate([v, v])[:, None]
    vecs = np.concatenate([columns(a["ln1_g"]), columns(a["ln1_b"]), columns(a["b_ada"]), columns(a["mlp_g"]), columns(a["mlp_b"]),
                           twice(a["qn_g"]), twice(a["qn_b"]), twice(a["kn_g"]), twice(a["kn_b"])], axis=1)
    fc1 = a["fc1s"].transpose(0, 2, 1).reshape(E, DC, P, DD).transpose(0, 2, 1, 3).reshape(E, P, DC * DD)
    fc2 = a["fc2s"].transpose(0, 2, 1).reshape(E, HC, P, D).transpose(0, 2, 1, 3).reshape(E, P, HC * D)
    b1 = a["b1s"].reshape(E, HC, P).transpose(0, 2, 1)
    p = np.arange(P)
    same = (p[:, None] % E == p[None, :] % E)
    consts = np.concatenate([np.eye(P), same, same & (p[:, None] < p[None, :]),
                             np.broadcast_to(np.arange(32), (P, 32)), p[:, None]], axis=1).astype(np.float32)
    arrays = {
        "x": a["x"],
        "condT": by_partition(a["cond_1024"].T),
        "w_adaT": by_partition(a["W_ada"].T),
        "vecs": np.ascontiguousarray(vecs),
        "w_qkvT": by_partition(a["Wqkv"].T),
        "w_outT": by_partition(a["Wout"].T),
        "w_gateT": by_partition(a["Wgate"].T),
        "experts": np.ascontiguousarray(np.concatenate([fc1, fc2, b1], axis=2)),
        "b2s": a["b2s"],
        "consts": consts,
    }
    nc = bacc.Bacc("TRN2", target_bir_lowering=False, num_devices=1)
    aps = [nc.dram_tensor(k, v.shape, F32, kind="ExternalInput").ap() for k, v in arrays.items()]
    out = nc.dram_tensor("out", (B, N, D), F32, kind="ExternalOutput").ap()
    build(nc, *aps, out)
    r = run_bass_kernel_spmd(nc, [arrays], core_ids=[0])
    return r.results[0]["out"]
```

```python
import numpy as np
import concourse.bass as bass
from concourse import mybir
from contextlib import ExitStack

F32 = mybir.dt.float32
F32R = mybir.dt.float32r
BF16 = mybir.dt.bfloat16
I32 = mybir.dt.int32
U32 = mybir.dt.uint32
ALU = mybir.AluOpType
ACT = mybir.ActivationFunctionType
AX = mybir.AxisListType

P = 128
B, N, D = 16, 256, 256
H, HD = 16, 64
E, DD = 8, 1024
TOK = B * N
CAP = TOK // E
EPS = 1e-5
TT = N // P
DC = D // P
HC = DD // P
UNITS = H // 2
GU = UNITS // 2
GW = GU * 2 * HD
TILES = TOK // P
KT = CAP // P
ROW = D + E
BIG = 4096.0
BITS = 30
NEWTON = 3
FIRST_LOOPED, LAST_LOOPED = 2, B - 2


CHUNKS = {(7, 0): ("q", 0), (7, 1): ("k", 0), (0, 0): ("q", 1), (0, 1): ("k", 1), (1, 0): ("v", 0), (1, 1): ("v", 1),
          (3, 0): ("q", 0), (3, 1): ("k", 0), (4, 0): ("q", 1), (4, 1): ("k", 1), (5, 0): ("v", 0), (5, 1): ("v", 1)}
ODD_STEPS = (0, 1, 7)


def group_of(b, hp):
    return b * 2 + (3 if hp == 7 else 1 if hp in ODD_STEPS else 2)


def batch_slots(b):
    cur, nxt, prv = 0 <= b < B, b + 1 < B, 1 <= b <= B
    out = [(hp, pos, name, "act") for (hp, pos), (name, _) in CHUNKS.items() if (cur if hp < 2 else nxt)]
    if prv:
        out += [(0, 2, "wout", "dve"), (6, 0, "tokT", "act"), (6, 1, "gate", "dve")]
    if nxt:
        out += [(1, 2, "xT", "act")]
    return sorted(out)


def make_counts():
    table, slots = {}, []
    totals = {}

    def hit(kind, b, key):
        totals[kind] = totals.get(kind, 0) + 1
        table[kind, b, key] = totals[kind]

    for b in range(-1, B + 1):
        cur, nxt, prv = 0 <= b < B, b + 1 < B, 1 <= b <= B
        for hp, pos, name, who in batch_slots(b):
            key = (hp, pos)
            hit("slot", b, key)
            hit(who, b, key)
            slots.append((b, key, who))
            if name in ("q", "k"):
                hit("chunk", b, key)
        for hp, live in ((0, cur or nxt), (4, nxt or prv)):
            if live:
                hit("newton", b, hp)
        for kind, live in (("x_loaded", nxt), ("xr_loaded", cur), ("tok_stored", prv)):
            if live:
                hit(kind, b, 0)
    for n, (b, key, who) in enumerate(slots):
        table["bank", b, key] = n % 2
        table["index", b, key] = n
        if n >= 2:
            pb, pkey, pwho = slots[n - 2]
            table["free", b, key] = (pwho, table[pwho, pb, pkey])
    return table


COUNTS = make_counts()


def through(kind, b, key):
    if isinstance(b, int):
        return COUNTS[kind, b, key]
    first, second = COUNTS[kind, FIRST_LOOPED, key], COUNTS[kind, FIRST_LOOPED + 1, key]
    step = second - first
    assert COUNTS[kind, LAST_LOOPED, key] == first + step * (LAST_LOOPED - FIRST_LOOPED)
    return b * step + (first - step * FIRST_LOOPED)


def bank_free(b, key):
    bi = b if isinstance(b, int) else FIRST_LOOPED + 1
    if ("free", bi, key) not in COUNTS:
        return None
    who, count = COUNTS["free", bi, key]
    if isinstance(b, int):
        return who, count
    who1, c1 = COUNTS["free", bi + 1, key]
    who0, c0 = COUNTS["free", bi - 1, key]
    assert who0 == who1 == who and c1 - count == count - c0
    return who, b * (c1 - count) + (count - (c1 - count) * bi)


def slot_bank(b, key):
    return COUNTS["bank", b if isinstance(b, int) else FIRST_LOOPED, key]


class Need:

    def __init__(self, eng):
        self.eng = eng

    def __call__(self, sem, count):
        if isinstance(count, int) and count <= 0:
            return
        self.eng.wait_ge(sem, count)


def over_batches(eng, batch):
    batch(-1, cur=False, nxt=True, prv=False)
    batch(0, cur=True, nxt=True, prv=False)
    batch(1, cur=True, nxt=True, prv=True)
    with eng.Fori(FIRST_LOOPED, LAST_LOOPED + 1) as b:
        batch(b, cur=True, nxt=True, prv=True)
    batch(B - 1, cur=True, nxt=False, prv=True)
    batch(B, cur=False, nxt=False, prv=True)


def build(nc, x, condT, w_adaT, vecs, w_qkvT, w_outT, w_gateT, experts, b2s, consts, out):
    ctx = ExitStack()
    with ctx:
        place = [ctx]

        def sb(name, shape, dt=F32):
            return place[0].enter_context(nc.sbuf_tensor(name, shape, dt))

        def ps(name, shape):
            return ctx.enter_context(nc.psum_tensor(name, shape, F32))

        def sem(name):
            return ctx.enter_context(nc.semaphore(name))

        rows_dram = nc.dram_tensor("rows_dram", [TOK, ROW], F32, kind="Internal").ap()
        list_dram = nc.dram_tensor("list_dram", [E * CAP], F32, kind="Internal").ap()

        NV = vecs.shape[1]
        NCON = consts.shape[1]
        vec = sb("vec", [P, NV])
        con = sb("con", [P, NCON])
        LN1_G, LN1_B, B_ADA, MLP_G, MLP_B, GQ, BQ, GK, BK = 0, 2, 4, 6, 8, 10, 11, 12, 13
        ident = con[:, 0:P]
        same_expert = con[:, P:2 * P]
        earlier_tile = con[:, 2 * P:3 * P]
        iota32 = con[:, 3 * P:3 * P + 32]
        partno = con[:, 3 * P + 32:3 * P + 33]
        tileno = iota32
        neg_ident = sb("neg_ident", [P, P], BF16)
        same_b = sb("same_b", [P, P], BF16)

        logit = sb("logit", [P, TILES, E])

        scope = ExitStack()
        place[0] = scope
        condT_sb = sb("condT_sb", [P, DC, B])
        sig = sb("sig", [P, DC, B])
        silu = sb("silu", [P, DC, B])
        wada_sb = sb("wada_sb", [P, DC, D])
        bias1 = sb("bias1", [P, DC, B])
        w_hi = sb("w_hi", [P, DC, 3 * H * HD], F32R)
        w_lo = sb("w_lo", [P, DC, 3 * H * HD], F32R)
        wo_sb = sb("wo_sb", [P, UNITS, D])
        wo_hi = sb("wo_hi", [P, UNITS, D], F32R)
        wo_lo = sb("wo_lo", [P, UNITS, D], F32R)
        wg_sb = sb("wg_sb", [P, DC, E])

        x_sb = sb("x_sb", [P, TT, D])
        xr_sb = sb("xr_sb", [P, TT, D])
        xh = sb("xh", [P, TT, D])
        hT = sb("hT", [P, DC, N])
        hT_hi = sb("hT_hi", [P, DC, N], F32R)
        hT_lo = sb("hT_lo", [P, DC, N], F32R)
        raw = sb("raw", [P, 4, GW])
        sq = [sb(f"sq{i}", [P, GW]) for i in range(2)]
        qn = [sb(f"qn{i}", [P, 4, GW]) for i in range(2)]
        NH = 4 * GU * 2
        ssum = sb("ssum", [P, NH])
        var = sb("var", [P, NH + 4])
        var_half = sb("var_half", [P, NH + 4], I32)
        ny = sb("ny", [P, NH + 4])
        na = sb("na", [P, NH + 4])
        rstd = [sb(f"rstd{i}", [P, NH + 4]) for i in range(2)]
        bn = sb("bn", [P, 4, 6])
        held_v = sb("held_v", [P, 1])
        held_p = sb("held_p", [P, 4])
        mv = sb("mv", [P, 4, 2])
        V = [sb(f"V{i}", [P, TT, GU * 256]) for i in range(2)]
        q_hi = [sb(f"q_hi{i}", [P, 2, N], F32R) for i in range(2)]
        q_lo = [sb(f"q_lo{i}", [P, 2, N], F32R) for i in range(2)]
        k_hi = [sb(f"k_hi{i}", [P, N], F32R) for i in range(2)]
        k_lo = [sb(f"k_lo{i}", [P, N], F32R) for i in range(2)]
        qkT = [sb(f"qkT{i}", [P, 2 * N]) for i in range(2)]
        m = [sb(f"m{i}", [P, 4], BF16) for i in range(2)]
        prob = [sb(f"prob{i}", [P, 2 * TT * N]) for i in range(2)]
        rowsum = sb("rowsum", [P, N])
        rec = sb("rec", [P, N])
        oT = [sb(f"oT{i}", [P, N]) for i in range(2)]
        o_hi = sb("o_hi", [P, UNITS, N], F32R)
        o_lo = sb("o_lo", [P, UNITS, N], F32R)
        tok = sb("tok", [P, TT, D])
        xh2 = sb("xh2", [P, TT, D])
        tokT = sb("tokT", [P, DC, N])
        scope.close()
        place[0] = ctx

        NP = 2 * P
        top = sb("top", [P, TILES])
        gates = sb("gates", [P, TILES, E])
        gT_ = sb("gates_T", [P, 2, P])
        hit = sb("hit", [P, NP], BF16)
        thr = sb("thr", [P, 1], I32)
        bit = sb("bit", [P, 1], I32)
        trial = sb("trial", [P, 1], I32)
        kept = sb("kept", [P, 1])
        cnt = sb("cnt", [P, 1], BF16)
        above = sb("above", [P, 2, P])
        equal = sb("equal", [P, 2, P])
        n4 = sb("n4", [P, 4])
        d4 = sb("d4", [P, 4])
        first4 = sb("first4", [P, 4])
        zeros = sb("zeros", [P, P])
        rank_a = sb("rank_a", [P, 2, P])
        rank_e = sb("rank_e", [P, 2, P])
        rank = sb("rank", [P, 2, P])
        rank_i = sb("rank_i", [P, TILES * E], I32)
        rank_hi = sb("rank_hi", [P, TILES * E], I32)
        rank_lo = sb("rank_lo", [P, TILES * E], I32)
        RA, RB = 32, 16
        one_a = sb("one_a", [P, TILES * E, RA], BF16)
        one_b = sb("one_b", [P, TILES * E, RB], BF16)
        val_b = sb("val_b", [P, TILES, 2, E // 4, 4 * RB], BF16)
        parts = sb("parts", [P, 2, 2, 4 * RB])
        index_a = sb("index_a", [P, 2, RB])
        lists = sb("lists", [E * KT, P])
        index = sb("index", [P, E * KT], I32)
        FC = DC * DD + HC * D + HC
        fcw = [sb(f"fcw{i}", [P, FC]) for i in range(2)]
        b2_sb = sb("b2_sb", [P, E, D])
        got = [sb(f"got{i}", [P, KT, ROW]) for i in range(2)]
        gT = sb("gT", [P, DC, CAP])
        yT = sb("yT", [P, HC, CAP])
        ysum = sb("ysum", [P, 2, D])
        yout = [sb(f"yout{i}", [P, KT, D]) for i in range(2)]

        pq = ps("pq", [P, 512])
        ch = [ps(f"ch{i}", [P, 512]) for i in range(2)]
        mx = ps("mx", [P, 1024])
        sc = ps("sc", [P, 1024])
        av = ps("av", [P, 512])

        con_in = sem("con_in")
        w_in = sem("w_in")
        wsmall_in = sem("wsmall_in")
        x_in = sem("x_in")
        xr_in = sem("xr_in")
        tok_out = sem("tok_out")
        row_out = sem("row_out")
        consts_ready = sem("consts_ready")
        tanh_done = sem("tanh_done")
        silu_ready = sem("silu_ready")
        shift_done = sem("shift_done")
        bias1_ready = sem("bias1_ready")
        w_ready = sem("w_ready")
        pads_ready = sem("pads_ready")
        qk_transposed = sem("qk_transposed")
        qk_evacuated = sem("qk_evacuated")
        hi_ready = sem("hi_ready")
        pre_scored = sem("pre_scored")
        max_ready = sem("max_ready")
        scored = sem("scored")
        prob_ready = sem("prob_ready")
        attended = sem("attended")
        normed = sem("normed")
        divided = sem("divided")
        qn_pool_ready = sem("qn_pool_ready")
        lo_ready = sem("lo_ready")
        k_split = sem("k_split")
        rowsum_ready = sem("rowsum_ready")
        o_split = sem("o_split")
        wo_ready = sem("wo_ready")
        slot_filled = sem("slot_filled")
        act_read = sem("act_read")
        dve_read = sem("dve_read")
        chunk_summed = sem("chunk_summed")
        rstd_ready = sem("rstd_ready")
        hT_ready = sem("hT_ready")
        hT_split = sem("hT_split")
        qn_ready = sem("qn_ready")
        xh_ready = sem("xh_ready")
        xh2_ready = sem("xh2_ready")
        dve_step = sem("dve_step")
        act_step = sem("act_step")
        pool_step = sem("pool_step")
        free_sem = {"act": act_read, "dve": dve_read}

        class Chain:

            def __init__(self, eng, semaphore, base=0):
                self.eng, self.sem, self.base, self.n = eng, semaphore, base, 0

            def count(self):
                return self.base + self.n

            def base_loop(self, base):
                self.kept, self.base = self.base, self.base + base

            def base_end(self, base):
                self.base = self.kept + base

            def __call__(self, ins):
                self.n += 1
                ins.then_inc(self.sem, 1)
                self.eng.wait_ge(self.sem, self.count())

        logits_ready = sem("logits_ready")
        exp_done = sem("exp_done")
        gates_ready = sem("gates_ready")
        gates_out = sem("gates_out")
        gates_transposed = sem("gates_transposed")
        counted_ready = sem("counted_ready")
        totals_ready = sem("totals_ready")
        n4_ready = sem("n4_ready")
        firsts_ready = sem("firsts_ready")
        rank_ready = sem("rank_ready")
        rank_transposed = sem("rank_transposed")
        hot_ready = sem("hot_ready")
        lists_ready = sem("lists_ready")
        index_a_ready = sem("index_a_ready")
        list_out = sem("list_out")
        list_in = sem("list_in")
        lists_transposed = sem("lists_transposed")
        index_ready = sem("index_ready")
        b2_in = sem("b2_in")
        fc_in = [sem(f"fc_in{i}") for i in range(2)]
        gathered = [sem(f"gathered{i}") for i in range(2)]
        scattered = sem("scattered")
        g_transposed = sem("g_transposed")
        gT_ready = sem("gT_ready")
        fc1_done = sem("fc1_done")
        gelu_done = sem("gelu_done")
        fc2_done = sem("fc2_done")
        fc2_read = sem("fc2_read")
        y_ready = sem("y_ready")

        block = ctx.enter_context(nc.Block())

        def wraw(c, v):
            if v == 0:
                return qn[c][:, :, :].rearrange("p a n -> p (a n)")
            return V[c][:, 0, :]

        def over_experts(eng, expert):
            with eng.Fori(0, E // 2 - 1) as i:
                expert(i * 2, 0, False)
                expert(i * 2 + 1, 1, False)
            expert(E - 2, 0, False)
            expert(E - 1, 1, True)

        def phase23_sync(sp):
            need = Need(sp)
            sp.wait_ge(logits_ready, 1)
            sp.dma_start(b2_sb[:, :, :].rearrange("p e d -> p (e d)"),
                         b2s.rearrange("(o e) d -> o (e d)", o=1).to_broadcast([P, E * D])).then_inc(b2_in, 16)

            def load(e, par):
                src = experts[e] if isinstance(e, int) else experts[bass.ds(e, 1)].rearrange("o p n -> p (o n)")
                sp.dma_start(fcw[par][:, :], src).then_inc(fc_in[par], 16)

            load(0, 0)
            load(1, 1)
            sp.wait_ge(gates_ready, 1)
            sp.dma_start(rows_dram[:, D:ROW].rearrange("(t p) e -> p t e", p=P), gates[:, :, :]).then_inc(gates_out, 16)
            sp.wait_ge(index_a_ready, 1)
            sp.dma_start(list_dram.rearrange("(h q b) -> q h b", h=2, b=RB), index_a[:, :, :]).then_inc(list_out, 16)
            sp.wait_ge(list_out, 16)
            sp.dma_start(lists[:, :], list_dram.rearrange("(m p) -> m p", p=P)).then_inc(list_in, 16)

            def expert(e, par, last):
                need(fc2_done, (e + 1) * KT)
                load(e + 2, par)
            with sp.Fori(0, E // 2 - 1) as i:
                expert(i * 2, 0, False)
                expert(i * 2 + 1, 1, False)

        def phase23_pool(pool):
            pool.wait_ge(index_ready, 1)
            pool.wait_ge(gates_out, 16)
            pool.wait_ge(row_out, B * 16)
            pool.wait_ge(tok_out, B * 16)

            def gather(e):
                par = e % 2
                if e >= 2:
                    pool.wait_ge(y_ready, e - 1)
                for k in range(KT):
                    nc.gpsimd.indirect_dma_start(
                        out=got[par][:, k, :], out_offset=None, in_=rows_dram,
                        in_offset=bass.IndirectOffsetOnAxis(ap=index[:, e * KT + k:e * KT + k + 1].bitcast(U32), axis=0),
                        compute_op=ALU.bypass).then_inc(gathered[par], 16)

            gather(0)
            gather(1)
            for e in range(E):
                pool.wait_ge(y_ready, e + 1)
                if e >= 1:
                    pool.wait_ge(scattered, 16 * KT * e)
                for k in range(KT):
                    nc.gpsimd.indirect_dma_start(
                        out=out.rearrange("b n d -> (b n) d"),
                        out_offset=bass.IndirectOffsetOnAxis(ap=index[:, e * KT + k:e * KT + k + 1].bitcast(U32), axis=0),
                        in_=yout[e % 2][:, k, :], in_offset=None,
                        compute_op=ALU.add).then_inc(scattered, 16)
                if e + 2 < E:
                    gather(e + 2)
            pool.wait_ge(scattered, 16 * KT * E)

        def phase23_scalar(act):
            act.wait_ge(logits_ready, 1)
            nc.scalar.activation(gates[:, :, :], gates[:, :, :], ACT.Exp).then_inc(exp_done, 1)

            def expert(e, par, last):
                act.wait_ge(g_transposed, e + 1)
                for c in range(DC):
                    ins = nc.scalar.activation(gT[:, c, :], mx[:, c * CAP:(c + 1) * CAP], ACT.Identity,
                                               bias=vec[:, MLP_B + c:MLP_B + c + 1], scale=vec[:, MLP_G + c:MLP_G + c + 1])
                ins.then_inc(gT_ready, 1)
                for hc in range(HC):
                    act.wait_ge(fc1_done, e * HC + hc + 1)
                    nc.scalar.activation(yT[:, hc, :], ch[hc % 2][:, :], ACT.Gelu_apprx_tanh,
                                         bias=fcw[par][:, FC - HC + hc:FC - HC + hc + 1]).then_inc(gelu_done, 1)
            over_experts(act, expert)

        def phase23_tensor(pe):
            pe.wait_ge(gates_ready, 1)
            for blk in range(2):
                ins = nc.tensor.transpose(mx[:, blk * P:(blk + 1) * P],
                                          gates[:, blk * 16:(blk + 1) * 16, :].rearrange("p t e -> p (t e)"), ident)
            ins.then_inc(gates_transposed, 1)
            with pe.Fori(0, BITS) as i:
                pe.wait_ge(counted_ready, i + 1)
                nc.tensor.matmul(av[:, 0:1], same_b[:, :], cnt[:, :], start=True, stop=True).then_inc(totals_ready, 1)
            pe.wait_ge(n4_ready, 1)
            nc.tensor.matmul(av[:, 4:8], earlier_tile, n4[:, :], start=True, stop=False)
            nc.tensor.matmul(av[:, 4:8], same_expert, d4[:, :], start=False, stop=True).then_inc(firsts_ready, 1)
            pe.wait_ge(rank_ready, 1)
            for blk in range(2):
                ins = nc.tensor.transpose(mx[:, 512 + blk * P:512 + (blk + 1) * P], rank[:, blk, :], ident)
            ins.then_inc(rank_transposed, 1)
            pe.wait_ge(hot_ready, 1)
            for t in range(TILES):
                for h in range(2):
                    ins = nc.tensor.matmul(ch[h][:, 0:P], one_a[:, t * E + 4 * h:t * E + 4 * h + 4, :].rearrange("p e a -> p (e a)"),
                                           val_b[:, t, :, h, :], start=(t == 0), stop=(t == TILES - 1))
            ins.then_inc(lists_ready, 1)

            pe.wait_ge(list_in, 16)
            nc.tensor.transpose(pq[:, 0:E * KT], lists[:, :], ident[0:E * KT, 0:E * KT]).then_inc(lists_transposed, 1)
            pe.wait_ge(gathered[0], 16 * KT)
            for c in range(DC):
                for k in range(KT):
                    ins = nc.tensor.transpose(mx[:, c * CAP + k * P:c * CAP + (k + 1) * P], got[0][:, k, c * P:(c + 1) * P], ident)
            ins.then_inc(g_transposed, 1)

            def expert(e, par, last, turn):
                w1 = fcw[par][:, 0:DC * DD].rearrange("p (c h) -> p c h", c=DC)
                w2 = fcw[par][:, DC * DD:DC * DD + HC * D].rearrange("p (c d) -> p c d", c=HC)
                pe.wait_ge(fc_in[par], (turn + 1) * 16)
                pe.wait_ge(gT_ready, e + 1)
                for hc in range(HC):
                    if not (isinstance(e, int) and e == 0 and hc < 2):
                        if hc < 2 and par == 0:
                            pe.wait_ge(gelu_done, e * HC)
                        else:
                            pe.wait_ge(gelu_done, e * HC + hc - 1)
                    for c in range(DC):
                        ins = nc.tensor.matmul(ch[hc % 2][:, :], w1[:, c, hc * P:(hc + 1) * P], gT[:, c, :], start=(c == 0), stop=(c == DC - 1))
                    ins.then_inc(fc1_done, 1)
                if not last:
                    pe.wait_ge(gathered[1 - par], (turn + 1 + par) * (16 * KT))
                    for c in range(DC):
                        for k in range(KT):
                            ins = nc.tensor.transpose(mx[:, c * CAP + k * P:c * CAP + (k + 1) * P], got[1 - par][:, k, c * P:(c + 1) * P], ident)
                    ins.then_inc(g_transposed, 1)
                pe.wait_ge(gelu_done, (e + 1) * HC)
                for k in range(KT):
                    bank = (av, pq)[k % 2]
                    if k < 2:
                        if not (isinstance(e, int) and e == 0):
                            pe.wait_ge(fc2_read, e * KT + k - 1)
                    else:
                        pe.wait_ge(fc2_read, e * KT + k - 1)
                    for hc in range(HC):
                        ins = nc.tensor.matmul(bank[:, 0:D], yT[:, hc, k * P:(k + 1) * P], w2[:, hc, :], start=(hc == 0), stop=(hc == HC - 1))
                    ins.then_inc(fc2_done, 1)

            expert(0, 0, False, 0)
            expert(1, 1, False, 0)
            with pe.Fori(1, E // 2 - 1) as i:
                expert(i * 2, 0, False, i)
                expert(i * 2 + 1, 1, False, i)
            expert(E - 2, 0, False, E // 2 - 1)
            expert(E - 1, 1, True, E // 2 - 1)

        def phase23_vector(dve, chain):
            need = Need(dve)
            V_ = nc.vector
            dve.wait_ge(dve_read, 2 * B)
            chain(V_.tensor_reduce(top[:, :], logit[:, :, :], AX.X, ALU.max))
            top3 = top[:, :].rearrange("p (t o) -> p t o", o=1).to_broadcast([P, TILES, E])
            V_.tensor_tensor(gates[:, :, :], logit[:, :, :], top3, ALU.subtract).then_inc(logits_ready, 1)
            dve.wait_ge(exp_done, 1)
            chain(V_.tensor_reduce(top[:, :], gates[:, :, :], AX.X, ALU.add))
            chain(V_.reciprocal(top[:, :], top[:, :]))
            V_.tensor_tensor(gates[:, :, :], gates[:, :, :], top3, ALU.mult).then_inc(gates_ready, 1)
            V_.memset(zeros[:, :], 0.0)
            V_.memset(d4[:, :], 0.0)
            V_.memset(bit[:, :], 1 << (BITS - 1))
            chain(V_.memset(thr[:, :], 0))
            dve.wait_ge(gates_transposed, 1)
            chain(V_.tensor_copy(gT_[:, :, :].rearrange("p b t -> p (b t)"), mx[:, 0:NP]))
            before = chain.n
            with dve.Fori(0, BITS) as i:
                chain.base_loop(i * 4)
                chain(V_.tensor_tensor(trial[:, :], thr[:, :], bit[:, :], ALU.bitwise_or))
                V_.tensor_scalar(hit[:, :], gT_[:, :, :].rearrange("p b t -> p (b t)"), trial[:, :].bitcast(F32), 0.0,
                                 ALU.is_ge, ALU.add, accum_out=cnt[:, :]).then_inc(counted_ready, 1)
                chain(V_.tensor_scalar(bit[:, :], bit[:, :], 1, None, ALU.logical_shift_right))
                dve.wait_ge(totals_ready, i + 1)
                chain(V_.scalar_tensor_tensor(kept[:, :], av[:, 0:1], CAP - 0.5, trial[:, :].bitcast(F32), ALU.is_ge, ALU.mult))
                chain(V_.tensor_tensor(thr[:, :].bitcast(F32), thr[:, :].bitcast(F32), kept[:, :], ALU.max))
            assert chain.n - before == 4
            chain.base_end(4 * (BITS - 1))
            t_ = thr[:, :].bitcast(F32)
            V_.tensor_scalar(above[:, :, :], gT_[:, :, :], t_, None, ALU.is_gt)
            chain(V_.tensor_scalar(equal[:, :, :], gT_[:, :, :], t_, None, ALU.is_equal))
            V_.tensor_reduce(n4[:, 0:2], above[:, :, :], AX.X, ALU.add)
            chain(V_.tensor_reduce(n4[:, 2:4], equal[:, :, :], AX.X, ALU.add))
            for i in range(3):
                ins = V_.tensor_tensor(d4[:, i + 1:i + 2], d4[:, i:i + 1], n4[:, i:i + 1], ALU.add)
                if i < 2:
                    chain(ins)
            ins.then_inc(n4_ready, 1)
            dve.wait_ge(firsts_ready, 1)
            chain(V_.tensor_scalar(first4[:, :], av[:, 4:8], -1.0, None, ALU.add))
            for blk in range(2):
                V_.tensor_tensor_scan(rank_a[:, blk, :], above[:, blk, :], zeros[:, :], first4[:, blk:blk + 1], ALU.add, ALU.add)
                ins = V_.tensor_tensor_scan(rank_e[:, blk, :], equal[:, blk, :], zeros[:, :], first4[:, 2 + blk:3 + blk], ALU.add, ALU.add)
            chain(ins)
            V_.tensor_tensor(rank_a[:, :, :], rank_a[:, :, :], above[:, :, :], ALU.mult)
            chain(V_.tensor_tensor(rank_e[:, :, :], rank_e[:, :, :], equal[:, :, :], ALU.mult))
            V_.tensor_tensor(rank_a[:, :, :], rank_a[:, :, :], rank_e[:, :, :], ALU.add)
            chain(V_.tensor_tensor(above[:, :, :], above[:, :, :], equal[:, :, :], ALU.add))
            chain(V_.tensor_scalar(above[:, :, :], above[:, :, :], -BIG, BIG, ALU.mult, ALU.add))
            V_.tensor_tensor(rank[:, :, :], rank_a[:, :, :], above[:, :, :], ALU.add).then_inc(rank_ready, 1)
            dve.wait_ge(rank_transposed, 1)
            chain(V_.tensor_copy(rank_i[:, :], mx[:, 512:512 + NP]))
            V_.tensor_scalar(rank_hi[:, :], rank_i[:, :], 4, None, ALU.logical_shift_right)
            chain(V_.tensor_scalar(rank_lo[:, :], rank_i[:, :], RB - 1, None, ALU.bitwise_and))
            TE = TILES * E

            def spread(ap, k):
                return ap.rearrange("p (n o) -> p n o", o=1).to_broadcast([P, TE, k])

            def ramp(k):
                return iota32[:, 0:k].rearrange("p (o k) -> p o k", o=1).to_broadcast([P, TE, k])
            V_.tensor_tensor(one_b[:, :, :], spread(rank_lo[:, :], RB), ramp(RB), ALU.is_equal)
            chain(V_.tensor_tensor(one_a[:, :, :], spread(rank_hi[:, :], RA), ramp(RA), ALU.is_equal))
            hot = one_b[:, :, :].rearrange("p (t h e) b -> p t h (e b)", t=TILES, h=2)
            V_.tensor_scalar(val_b[:, :, 0, :, :], hot, partno, None, ALU.mult)
            V_.tensor_tensor(val_b[:, :, 1, :, :].rearrange("p t h c -> p t (h c)") if False else val_b[:, :, 1, :, :], hot,
                             tileno.rearrange("p (t o q) -> p t o q", o=1, q=1).to_broadcast([P, TILES, 2, 4 * RB]), ALU.mult).then_inc(hot_ready, 1)
            dve.wait_ge(lists_ready, 1)
            for h in range(2):
                ins = V_.tensor_copy(parts[:, h, :, :].rearrange("p v c -> p (v c)"), ch[h][:, 0:P])
            chain(ins)
            for h in range(2):
                for e in range(4):
                    q = slice(32 * e, 32 * e + 32)
                    ins = V_.scalar_tensor_tensor(index_a[q, h, :], parts[q, h, 1, e * RB:(e + 1) * RB], float(P),
                                                  parts[q, h, 0, e * RB:(e + 1) * RB], ALU.mult, ALU.add)
            ins.then_inc(index_a_ready, 1)
            dve.wait_ge(lists_transposed, 1)
            V_.tensor_copy(index[:, :], pq[:, 0:E * KT]).then_inc(index_ready, 1)

            dve.wait_ge(b2_in, 16)

            def expert(e, par, last):
                for k in range(KT):
                    dve.wait_ge(fc2_done, e * KT + k + 1)
                    if k == 0 and not (isinstance(e, int) and e < 2):
                        dve.wait_ge(scattered, (e - 1) * (16 * KT))
                    b2 = (b2_sb[:, e, :] if isinstance(e, int) else
                          b2_sb[:, :, :].rearrange("p e d -> p (e d)")[:, bass.ds(e * D, D)])
                    w = (got[par][:, k, D + e:D + e + 1] if isinstance(e, int) else got[par][:, k, bass.ds(e + D, 1)])
                    ins = V_.tensor_tensor(ysum[:, k % 2, :], (av, pq)[k % 2][:, 0:D], b2, ALU.add)
                    ins.then_inc(fc2_read, 1)
                    dve.wait_ge(fc2_read, e * KT + k + 1)
                    ins = V_.tensor_scalar(yout[par][:, k, :], ysum[:, k % 2, :], w, None, ALU.mult)
                ins.then_inc(y_ready, 1)
            expert(0, 0, False)
            expert(1, 1, False)
            with dve.Fori(1, E // 2) as i:
                expert(i * 2, 0, False)
                expert(i * 2 + 1, 1, False)

        POOL_CHUNKS = 2

        def times_rstd(eng, par, c):
            r = rstd[par][:, c * 8:(c + 1) * 8].rearrange("p (h o) -> p h o", o=1).to_broadcast([P, 8, HD])
            return eng.tensor_tensor(qn[par][:, c, :].rearrange("p (h d) -> p h d", d=HD),
                                     raw[:, c, :].rearrange("p (h d) -> p h d", d=HD), r, ALU.mult)

        def sync_batch(sp):
            need = Need(sp)

            def batch(b, cur, nxt, prv):
                if nxt:
                    need(xh_ready, b + 1)
                    sp.dma_start(x_sb[:, :, :], x[bass.ds(b + 1, 1)].rearrange("o (t p) d -> p (o t) d", p=P)
                                 if not isinstance(b, int) else x[b + 1].rearrange("(t p) d -> p t d", p=P)).then_inc(x_in, 16)
                if prv:
                    need(dve_read, through("dve", b, (0, 2)))
                    dst = (out[bass.ds(b - 1, 1)].rearrange("o (t p) d -> p (o t) d", p=P)
                           if not isinstance(b, int) else out[b - 1].rearrange("(t p) d -> p t d", p=P))
                    sp.dma_start(dst, tok[:, :, :]).then_inc(tok_out, 16)
                if cur:
                    src = (x[bass.ds(b, 1)].rearrange("o (t p) d -> p (o t) d", p=P)
                           if not isinstance(b, int) else x[b].rearrange("(t p) d -> p t d", p=P))
                    sp.dma_start(xr_sb[:, :, :], src).then_inc(xr_in, 16)
                if prv:
                    need(xh2_ready, b)
                    r = (rows_dram[bass.ds((b - 1) * N, N)] if not isinstance(b, int)
                         else rows_dram[(b - 1) * N:b * N])
                    sp.dma_start(r[:, 0:D].rearrange("(t p) d -> p t d", p=P), xh2[:, :, :]).then_inc(row_out, 16)
            return batch

        @block.sync
        def _(sp):
            sp.dma_start(con[:, :], consts).then_inc(con_in, 16)
            sp.dma_start(vec[:, :], vecs).then_inc(con_in, 16)
            sp.dma_start(condT_sb[:, :, :], condT).then_inc(con_in, 16)
            sp.dma_start(wada_sb[:, :, :], w_adaT).then_inc(con_in, 16)
            for c in range(DC):
                sp.dma_start(wraw(c, 0), w_qkvT[:, c, 0:2048]).then_inc(w_in, 16)
                sp.dma_start(wraw(c, 1), w_qkvT[:, c, 2048:3072]).then_inc(w_in, 16)
            sp.dma_start(wo_sb[:, :, :], w_outT).then_inc(wsmall_in, 16)
            sp.dma_start(wg_sb[:, :, :], w_gateT).then_inc(wsmall_in, 16)
            over_batches(sp, sync_batch(sp))
            phase23_sync(sp)

        @block.gpsimd
        def _(pool):
            need = Need(pool)
            for i in range(2):
                nc.gpsimd.memset(q_hi[i][:, :, :].bitcast(F32), 0.0).then_inc(pads_ready, 1)
                nc.gpsimd.memset(q_lo[i][:, :, :].bitcast(F32), 0.0).then_inc(pads_ready, 1)
            pool.wait_ge(w_ready, 1)
            for i in range(2):
                for jt in range(TT):
                    ones = V[i][:, jt, :].rearrange("p (u c) -> p u c", c=256)[:, :, HD:HD + 128]
                    nc.gpsimd.memset(ones, 1.0).then_inc(pads_ready, 1)
            pool.wait_ge(wsmall_in, 32)
            nc.gpsimd.tensor_copy(wo_hi[:, :, :], wo_sb[:, :, :]).then_inc(wo_ready, 1)
            pool.wait_ge(wo_ready, 1)
            nc.gpsimd.tensor_tensor(wo_lo[:, :, :], wo_sb[:, :, :], wo_hi[:, :, :].bitcast(F32), ALU.subtract).then_inc(wo_ready, 1)

            def batch(b, cur, nxt, prv):
                def normalise(hp, c):
                    par = 1 if hp == 0 else 0
                    g = b * 2 + (1 if hp == 0 else 2)
                    if c == 0:
                        need(rstd_ready, through("newton", b, hp))
                        need(qk_transposed, (g - 1) * GU)
                    ins = times_rstd(nc.gpsimd, par, c)
                    if c == POOL_CHUNKS - 1:
                        ins.then_inc(qn_pool_ready, 1)

                for hp in range(UNITS):
                    u = b * UNITS + hp
                    par = (hp + 1) % 2
                    if (cur and nxt) or (cur and hp < UNITS - 1) or (nxt and hp == UNITS - 1):
                        need(qk_evacuated, u + 2)
                        need(scored, u)
                        f, lo, hi = qkT[par], q_lo[par], q_hi[par]
                        nc.gpsimd.tensor_tensor(k_lo[par][:, :], f[:, N:2 * N], k_hi[par][:, :].bitcast(F32), ALU.subtract).then_inc(k_split, 1)
                        nc.gpsimd.tensor_tensor(lo[0:64, 0, :], f[0:64, 0:N], hi[0:64, 0, :].bitcast(F32), ALU.subtract)
                        need(k_split, u + 2)
                        nc.gpsimd.tensor_tensor(lo[64:128, 1, :], f[64:128, 0:N], hi[64:128, 1, :].bitcast(F32), ALU.subtract).then_inc(lo_ready, 1)
                        need(lo_ready, u + 2)
                        nc.gpsimd.tensor_tensor(held_p[:, 3:4], partno, partno, ALU.add)
                    if (cur and hp > 0) or (hp == 0 and prv):
                        pair = (hp - 1) % UNITS
                        need(normed, u)
                        nc.gpsimd.tensor_tensor(o_lo[:, pair, :], oT[(hp - 1) % 2][:, :], o_hi[:, pair, :].bitcast(F32), ALU.subtract).then_inc(o_split, 1)
                    if hp in (0, 1) and cur:
                        normalise(0, hp)
                    if hp in (4, 5) and nxt:
                        normalise(4, hp - 4)

            over_batches(pool, batch)
            phase23_pool(pool)

        @block.scalar
        def _(act):
            need = Need(act)
            act.wait_ge(con_in, 64)
            nc.scalar.activation(sig[:, :, :], condT_sb[:, :, :], ACT.Tanh, scale=0.5).then_inc(tanh_done, 1)

            def chunk(b, hp, pos):
                key = (hp, pos)
                bank = ch[slot_bank(b, key)]
                name, t = CHUNKS[key]
                g = group_of(b, hp)
                need(slot_filled, through("slot", b, key))
                if name != "v":
                    c = 2 * t + pos
                    need(qn_ready if c >= POOL_CHUNKS else qn_pool_ready, g)
                    nc.scalar.activation(raw[:, c, :], bank[:, :], ACT.Copy)
                    need(chunk_summed, through("chunk", b, key) - 2)
                    nc.scalar.activation(sq[c % 2][:, :], bank[:, :], ACT.Square).then_inc(act_read, 1)
                else:
                    need(attended, (g - 1) * GU)
                    dst = V[1 if hp in ODD_STEPS else 0][:, t, :].rearrange("p (u a c) -> p u a c", u=GU, a=4)
                    src = bank[:, :].rearrange("p (u a c) -> p u a c", u=GU, a=2)
                    nc.scalar.activation(dst[:, :, 0:4:3, :], src, ACT.Copy).then_inc(act_read, 1)

            def batch(b, cur, nxt, prv):
                for hp in range(UNITS):
                    u = b * UNITS + hp
                    par = (hp + 1) % 2
                    ahead = (cur and nxt) or (cur and hp < UNITS - 1) or (nxt and hp == UNITS - 1)
                    live = (hp, 0) in CHUNKS and (cur if hp < 2 else nxt)
                    if ahead:
                        need(qk_transposed, u + 2)
                        need(scored, u)
                        if isinstance(b, int) and b < 0:
                            need(pads_ready, 4)
                        nc.scalar.activation(q_hi[par][0:64, 0, :], pq[0:64, 0:N], ACT.Identity,
                                             bias=vec[0:64, BQ:BQ + 1], scale=vec[0:64, GQ:GQ + 1])
                        nc.scalar.activation(q_hi[par][64:128, 1, :], pq[64:128, 0:N], ACT.Identity,
                                             bias=vec[64:128, BQ:BQ + 1], scale=vec[64:128, GQ:GQ + 1])
                        nc.scalar.activation(k_hi[par][:, :], pq[:, N:2 * N], ACT.Identity,
                                             bias=vec[:, BK:BK + 1], scale=vec[:, GK:GK + 1]).then_inc(hi_ready, 1)
                        need(lo_ready, u)
                        nc.scalar.activation(qkT[par][:, 0:N], pq[:, 0:N], ACT.Identity,
                                             bias=vec[:, BQ:BQ + 1], scale=vec[:, GQ:GQ + 1])
                        nc.scalar.activation(qkT[par][:, N:2 * N], pq[:, N:2 * N], ACT.Identity,
                                             bias=vec[:, BK:BK + 1], scale=vec[:, GK:GK + 1]).then_inc(qk_evacuated, 1)
                    if live:
                        chunk(b, hp, 0)
                    if hp == 6 and prv:
                        need(slot_filled, through("slot", b, (6, 0)))
                        nc.scalar.activation(tokT[:, :, :].rearrange("p c n -> p (c n)"),
                                             ch[slot_bank(b, (6, 0))][:, :], ACT.Copy).then_inc(act_read, 1)
                    if (cur and hp > 0) or (hp == 0 and prv):
                        need(attended, u)
                        need(divided, u - 1)
                        nc.scalar.activation(rowsum[0:64, :], av[64:128, 0:N], ACT.Copy)
                        nc.scalar.activation(rowsum[64:128, :], av[0:64, N:2 * N], ACT.Copy).then_inc(rowsum_ready, 1)
                    if cur:
                        need(scored, u + 1)
                        need(attended, u - 1)
                        nc.scalar.activation(prob[hp % 2][:, :], sc[:, :], ACT.Exp, scale=HD ** -0.5).then_inc(prob_ready, 1)
                    if live:
                        chunk(b, hp, 1)
                    if hp == 1 and nxt:
                        need(slot_filled, through("slot", b, (1, 2)))
                        need(bias1_ready, 1)
                        need(hT_split, b + 1)
                        bank = ch[slot_bank(b, (1, 2))]
                        for c in range(DC):
                            bias = (bias1[:, c, b + 1:b + 2] if isinstance(b, int) else bias1[:, c, bass.ds(b + 1, 1)])
                            ins = nc.scalar.activation(hT[:, c, :], bank[:, c * N:(c + 1) * N], ACT.Identity,
                                                       bias=bias, scale=vec[:, LN1_G + c:LN1_G + c + 1])
                        ins.then_inc(act_read, 1)

            over_batches(act, batch)
            phase23_scalar(act)

        def rsqrt(chain, n, dst):
            v, y, a = var[:, 0:n], ny[:, 0:n], na[:, 0:n]
            half = var_half[:, 0:n]
            chain(nc.vector.tensor_scalar(half, v.bitcast(I32), 1, None, ALU.logical_shift_right))
            chain(nc.vector.tensor_scalar(y.bitcast(I32), half, -1.0, float(0x5F3759DF), ALU.mult, ALU.add))
            for r in range(NEWTON):
                chain(nc.vector.scalar_tensor_tensor(a, y, -0.5, y, ALU.mult, ALU.mult))
                chain(nc.vector.tensor_tensor(a, a, v, ALU.mult))
                if r < NEWTON - 1:
                    chain(nc.vector.scalar_tensor_tensor(y, a, 1.5, y, ALU.add, ALU.mult))
                else:
                    nc.vector.scalar_tensor_tensor(dst[:, 0:n], a, 1.5, y, ALU.add, ALU.mult).then_inc(rstd_ready, 1)

        @block.vector
        def _(dve):
            need = Need(dve)
            chain = Chain(dve, dve_step)
            dve.wait_ge(con_in, 64)
            nc.vector.tensor_scalar(neg_ident[:, :], ident, -1.0, None, ALU.mult).then_inc(consts_ready, 1)
            nc.vector.tensor_copy(same_b[:, :], same_expert).then_inc(consts_ready, 1)
            nc.vector.memset(mv[:, :, :], 1.0)
            chain(nc.vector.memset(var[:, :], 1.0))
            dve.wait_ge(tanh_done, 1)
            chain(nc.vector.scalar_tensor_tensor(sig[:, :, :], sig[:, :, :], 1.0, condT_sb[:, :, :], ALU.add, ALU.mult))
            nc.vector.tensor_scalar(silu[:, :, :], sig[:, :, :], 0.5, None, ALU.mult).then_inc(silu_ready, 1)
            dve.wait_ge(shift_done, 1)
            for c in range(DC):
                ins = nc.vector.tensor_scalar(bias1[:, c, :], av[:, c * B:(c + 1) * B], vec[:, B_ADA + c:B_ADA + c + 1],
                                              vec[:, LN1_B + c:LN1_B + c + 1], ALU.add, ALU.add)
            ins.then_inc(bias1_ready, 1)
            dve.wait_ge(w_in, 2 * DC * 16)
            for c in range(DC):
                wqk = wraw(c, 0)
                means = raw[:, c, 0:2 * H]
                w3 = wqk.rearrange("p (h d) -> p h d", d=HD)
                chain(nc.vector.tensor_reduce(means, w3, AX.X, ALU.add))
                chain(nc.vector.tensor_scalar(means, means, 1.0 / HD, None, ALU.mult))
                chain(nc.vector.tensor_tensor(w3, w3, means.rearrange("p (h o) -> p h o", o=1).to_broadcast([P, 2 * H, HD]), ALU.subtract))
                for a, bb, src in ((0, 2048, wqk), (2048, 3072, wraw(c, 1))):
                    chain(nc.vector.tensor_copy(w_hi[:, c, a:bb], src))
                    ins = nc.vector.tensor_tensor(w_lo[:, c, a:bb], src, w_hi[:, c, a:bb].bitcast(F32), ALU.subtract)
            ins.then_inc(w_ready, 1)

            def row_stats(rows, at):
                for t in range(TT):
                    ins = nc.vector.bn_stats(bn[:, at + t, :], rows[:, t, :])
                ins.then_inc(dve_step, 1)
                chain.n += 1
                dve.wait_ge(dve_step, chain.count())
                nc.vector.memset(held_v[:, :], 0.0)
                for t in range(TT):
                    ins = nc.vector.bn_aggr(mv[:, at + t, :], bn[:, at + t, :])
                chain(ins)

            def head_sums(b, hp, pos):
                name, t = CHUNKS[hp, pos]
                c = 2 * t + pos
                need(act_read, through("act", b, (hp, pos)))
                nc.vector.tensor_reduce(ssum[:, c * 8:(c + 1) * 8],
                                        sq[c % 2][:, :].rearrange("p (h d) -> p h d", d=HD), AX.X, ALU.add).then_inc(chunk_summed, 1)

            def batch(b, cur, nxt, prv):
                for hp in range(UNITS):
                    u = b * UNITS + hp
                    if hp == 1 and prv:
                        need(slot_filled, through("slot", b, (0, 2)))
                        need(xr_in, b * 16)
                        need(tok_out, (b - 1) * 16)
                        need(xh2_ready, b - 1)
                        nc.vector.tensor_tensor(tok[:, :, :].rearrange("p t d -> p (t d)"), ch[slot_bank(b, (0, 2))][:, :],
                                                xr_sb[:, :, :].rearrange("p t d -> p (t d)"), ALU.add).then_inc(dve_read, 1)
                    if hp == 2 and nxt:
                        need(act_read, through("act", b, (1, 2)))
                        chain(nc.vector.tensor_copy(hT_hi[:, :, :], hT[:, :, :]))
                        nc.vector.tensor_tensor(hT_lo[:, :, :], hT[:, :, :], hT_hi[:, :, :].bitcast(F32), ALU.subtract).then_inc(hT_split, 1)
                    if hp == 1 and nxt:
                        need(rstd_ready, through("newton", b, 0))
                        if cur:
                            need(slot_filled, through("slot", b - 1, (1, 2)))
                        for t in range(TT):
                            ins = nc.vector.tensor_scalar(xh[:, t, :], x_sb[:, t, :], mv[:, t, 0:1],
                                                          rstd[1][:, NH + t:NH + t + 1], ALU.subtract, ALU.mult)
                        ins.then_inc(xh_ready, 1)
                    if (cur and hp > 0) or (hp == 0 and prv):
                        need(rowsum_ready, u)
                        need(divided, u - 1)
                        need(o_split, u - 2)
                        chain(nc.vector.reciprocal(rec[:, :], rowsum[:, :]))
                        o = oT[(hp - 1) % 2]
                        nc.vector.tensor_tensor(o[0:64, :], av[0:64, 0:N], rec[0:64, :], ALU.mult)
                        nc.vector.tensor_tensor(o[64:128, :], av[64:128, N:2 * N], rec[64:128, :], ALU.mult).then_inc(divided, 1)
                        need(divided, u)
                        if hp == 1 and prv:
                            need(slot_filled, through("slot", b, (0, 2)))
                        nc.vector.tensor_copy(o_hi[:, (hp - 1) % UNITS, :], o[:, :]).then_inc(normed, 1)
                    if hp == 0 and nxt:
                        need(x_in, (b + 2) * 16)
                        row_stats(x_sb, 0)
                    if hp in (0, 3, 4, 7) and (cur if hp < 2 else nxt):
                        head_sums(b, hp, 0)
                        head_sums(b, hp, 1)
                    if hp == 6 and prv:
                        need(slot_filled, through("slot", b, (6, 1)))
                        dst = (logit[:, (b - 1) * TT:b * TT, :].rearrange("p t e -> p (t e)") if isinstance(b, int)
                               else logit[:, :, :].rearrange("p t e -> p (t e)")[:, bass.ds((b - 1) * TT * E, TT * E)])
                        nc.vector.tensor_copy(dst, ch[slot_bank(b, (6, 1))][:, 0:TT * E]).then_inc(dve_read, 1)
                    if (cur and nxt) or (cur and hp < UNITS - 1) or (nxt and hp == UNITS - 1):
                        need(pre_scored, u + 2)
                        need(scored, u)
                        nc.vector.tensor_reduce(m[(hp + 1) % 2][:, :], mx[:, :].rearrange("p (a j) -> p a j", a=4),
                                                AX.X, ALU.max).then_inc(max_ready, 1)
                    if hp == 5 and prv:
                        need(rstd_ready, through("newton", b, 4))
                        need(row_out, (b - 1) * 16)
                        for t in range(TT):
                            ins = nc.vector.tensor_scalar(xh2[:, t, :], tok[:, t, :], mv[:, 2 + t, 0:1],
                                                          rstd[0][:, NH + 2 + t:NH + 3 + t], ALU.subtract, ALU.mult)
                        ins.then_inc(xh2_ready, 1)
                    if (hp == 1 and cur) or (hp == 5 and nxt):
                        g = b * 2 + (1 if hp == 1 else 2)
                        need(rstd_ready, through("newton", b, hp - 1))
                        need(qk_transposed, (g - 1) * GU)
                        for c in range(POOL_CHUNKS, 4):
                            ins = times_rstd(nc.vector, 1 if hp == 1 else 0, c)
                        ins.then_inc(qn_ready, 1)
                    if hp == 2 and prv:
                        need(dve_read, through("dve", b, (0, 2)))
                        row_stats(tok, 2)
                    if (hp == 0 and (cur or nxt)) or (hp == 4 and (nxt or prv)):
                        if cur if hp == 0 else nxt:
                            need(chunk_summed, through("chunk", b, (hp, 1)))
                            chain(nc.vector.tensor_scalar(var[:, 0:NH], ssum[:, :], 1.0 / HD, EPS, ALU.mult, ALU.add))
                        at = 0 if hp == 0 else 2
                        chain(nc.vector.tensor_scalar(var[:, NH + at:NH + at + 2], mv[:, at:at + 2, 1], EPS, None, ALU.add))
                        if hp == 0 and cur:
                            need(qn_pool_ready, b * 2)
                        if hp == 4 and (cur or nxt):
                            need(qn_pool_ready, b * 2 + 1)
                        rsqrt(chain, NH + at + 2, rstd[1 if hp == 0 else 0])


            per = 37
            def counted(b, cur, nxt, prv):
                before = chain.n
                if not isinstance(b, int):
                    chain.base = (b - FIRST_LOOPED) * per
                batch(b, cur, nxt, prv)
                if not isinstance(b, int):
                    assert chain.n - before == per, chain.n - before
                    chain.base = per * (LAST_LOOPED - FIRST_LOOPED)
            over_batches(dve, counted)
            phase23_vector(dve, chain)

        def three_passes(psum, l_hi, l_lo, r_hi, r_lo, first, last):
            nc.tensor.matmul(psum, l_lo, r_hi, start=first, stop=False)
            nc.tensor.matmul(psum, l_hi, r_lo, start=False, stop=False)
            return nc.tensor.matmul(psum, l_hi, r_hi, start=False, stop=last)

        @block.tensor
        def _(pe):
            need = Need(pe)
            pe.wait_ge(con_in, 64)
            pe.wait_ge(silu_ready, 1)
            for mc in range(DC):
                for c in range(DC):
                    ins = nc.tensor.matmul(av[:, mc * B:(mc + 1) * B], wada_sb[:, c, mc * P:(mc + 1) * P], silu[:, c, :],
                                           start=(c == 0), stop=(c == DC - 1))
            ins.then_inc(shift_done, 1)
            pe.wait_ge(consts_ready, 2)

            def take_bank(b, key):
                free = bank_free(b, key)
                if free:
                    need(free_sem[free[0]], free[1])
                return ch[slot_bank(b, key)]

            def chunk(b, hp, pos):
                bank = take_bank(b, (hp, pos))
                name, t = CHUNKS[hp, pos]
                if pos == 0:
                    need(hT_split, b + 1 if hp < 2 else b + 2)
                if isinstance(b, int) and b < 0 and hp == 3 and pos == 0:
                    need(w_ready, 1)
                col = "qkv".index(name) * H * HD + (GW if hp in ODD_STEPS else 0)
                for c in range(DC):
                    ins = three_passes(bank[:, :], hT_hi[:, c, t * P:(t + 1) * P], hT_lo[:, c, t * P:(t + 1) * P],
                                       w_hi[:, c, col:col + GW], w_lo[:, c, col:col + GW], c == 0, c == DC - 1)
                ins.then_inc(slot_filled, 1)

            def transposed(bank, rows):
                for c in range(DC):
                    for t in range(TT):
                        ins = nc.tensor.transpose(bank[:, c * N + t * P:c * N + (t + 1) * P], rows[:, t, c * P:(c + 1) * P], ident)
                ins.then_inc(slot_filled, 1)

            def batch(b, cur, nxt, prv):
                for hp in range(UNITS):
                    u = b * UNITS + hp
                    ahead = (cur and nxt) or (cur and hp < UNITS - 1) or (nxt and hp == UNITS - 1)
                    npar = (hp + 1) % 2
                    live = (hp, 0) in CHUNKS and (cur if hp < 2 else nxt)
                    if ahead:
                        gpar, i = ((hp + 1) // GU) % 2, (hp + 1) % GU
                        need(qn_ready, b * 2 + (hp + 1) // GU + 1)
                        need(qn_pool_ready, b * 2 + (hp + 1) // GU + 1)
                        need(qk_evacuated, u + 1)
                        for c, at in ((0, 0), (2, 1), (1, 2), (3, 3)):
                            ins = nc.tensor.transpose(pq[:, at * P:(at + 1) * P], qn[gpar][:, c, i * P:(i + 1) * P], ident)
                        ins.then_inc(qk_transposed, 1)
                    if live:
                        chunk(b, hp, 0)
                    if hp == 6 and prv:
                        bank = take_bank(b, (6, 0))
                        need(dve_read, through("dve", b, (0, 2)))
                        transposed(bank, tok)
                    if (cur and hp > 0) or (hp == 0 and prv):
                        need(prob_ready, u)
                        need(divided, u - 1)
                        i = (hp - 1) % GU
                        gpar = ((hp - 1) // GU) % 2
                        if i == 0:
                            need(act_read, through("act", b, (1, 1)) if hp == 5 else through("act", b, (0, 0)) - 1)
                            if isinstance(b, int) and b == 0:
                                need(pads_ready, 8)
                        for hh in range(2):
                            for jt in range(TT):
                                ins = nc.tensor.matmul(av[:, hh * N:(hh + 1) * N], V[gpar][:, jt, i * 256 + hh * P:i * 256 + (hh + 1) * P],
                                                       prob[(hp - 1) % 2][:, hh * TT * N + jt * N:hh * TT * N + (jt + 1) * N],
                                                       start=(jt == 0), stop=(jt == TT - 1))
                        ins.then_inc(attended, 1)
                    if cur:
                        need(prob_ready, u)
                        need(max_ready, u + 1)
                        need(lo_ready, u + 1)
                        par = hp % 2
                        for hh in range(2):
                            for jt in range(TT):
                                at = hh * TT * N + jt * N
                                keys = slice(jt * P, (jt + 1) * P)
                                three_passes(sc[:, at:at + N], k_hi[par][:, keys], k_lo[par][:, keys],
                                             q_hi[par][:, hh, :], q_lo[par][:, hh, :], True, False)
                                for it in range(TT):
                                    ins = nc.tensor.matmul(sc[:, at + it * P:at + (it + 1) * P],
                                                           m[par][:, it * 2 + hh:it * 2 + hh + 1].to_broadcast([P, P]),
                                                           neg_ident[:, :], start=False, stop=(it == TT - 1))
                        ins.then_inc(scored, 1)
                    if live:
                        chunk(b, hp, 1)
                    if hp == 1 and nxt:
                        bank = take_bank(b, (1, 2))
                        need(xh_ready, b + 2)
                        transposed(bank, xh)
                    if hp == 6 and prv:
                        bank = take_bank(b, (6, 1))
                        need(act_read, through("act", b, (6, 0)))
                        for t in range(TT):
                            for c in range(DC):
                                ins = nc.tensor.matmul(bank[:, t * E:(t + 1) * E], tokT[:, c, t * P:(t + 1) * P], wg_sb[:, c, :],
                                                       start=(c == 0), stop=(c == DC - 1))
                        ins.then_inc(slot_filled, 1)
                    if ahead:
                        need(hi_ready, u + 2)
                        need(max_ready, u + 1)
                        for it in range(TT):
                            for hh in range(2):
                                at = (it * 2 + hh) * N
                                ins = nc.tensor.matmul(mx[:, at:at + N], q_hi[npar][:, hh, it * P:(it + 1) * P], k_hi[npar][:, :],
                                                       start=True, stop=True)
                        ins.then_inc(pre_scored, 1)
                    if hp == 0 and prv:
                        bank = take_bank(b, (0, 2))
                        need(o_split, u - 1)
                        if isinstance(b, int) and b == 1:
                            need(wo_ready, 2)
                        for t in range(TT):
                            for pair in range(UNITS):
                                if t == 0 and pair == UNITS - 1:
                                    need(o_split, u)
                                ins = three_passes(bank[:, t * D:(t + 1) * D], o_hi[:, pair, t * P:(t + 1) * P], o_lo[:, pair, t * P:(t + 1) * P],
                                                   wo_hi[:, pair, :], wo_lo[:, pair, :], pair == 0, pair == UNITS - 1)
                        ins.then_inc(slot_filled, 1)

            over_batches(pe, batch)
            phase23_tensor(pe)


def kernel(**inputs):
    import concourse.bacc as bacc
    from concourse.bass_utils import run_bass_kernel_spmd

    a = {k.removeprefix("L0_cond_"): np.asarray(v) for k, v in inputs.items()}

    def by_partition(w):
        return np.ascontiguousarray(w.reshape(-1, P, w.shape[-1]).transpose(1, 0, 2))

    def columns(v):
        return v.reshape(-1, P).T

    twice = lambda v: np.concatenate([v, v])[:, None]
    vecs = np.concatenate([columns(a["ln1_g"]), columns(a["ln1_b"]), columns(a["b_ada"]), columns(a["mlp_g"]), columns(a["mlp_b"]),
                           twice(a["qn_g"]), twice(a["qn_b"]), twice(a["kn_g"]), twice(a["kn_b"])], axis=1)
    fc1 = a["fc1s"].transpose(0, 2, 1).reshape(E, DC, P, DD).transpose(0, 2, 1, 3).reshape(E, P, DC * DD)
    fc2 = a["fc2s"].transpose(0, 2, 1).reshape(E, HC, P, D).transpose(0, 2, 1, 3).reshape(E, P, HC * D)
    b1 = a["b1s"].reshape(E, HC, P).transpose(0, 2, 1)
    p = np.arange(P)
    same = (p[:, None] % E == p[None, :] % E)
    consts = np.concatenate([np.eye(P), same, same & (p[:, None] < p[None, :]),
                             np.broadcast_to(np.arange(32), (P, 32)), p[:, None]], axis=1).astype(np.float32)
    arrays = {
        "x": a["x"],
        "condT": by_partition(a["cond_1024"].T),
        "w_adaT": by_partition(a["W_ada"].T),
        "vecs": np.ascontiguousarray(vecs),
        "w_qkvT": by_partition(a["Wqkv"].T),
        "w_outT": by_partition(a["Wout"].T),
        "w_gateT": by_partition(a["Wgate"].T),
        "experts": np.ascontiguousarray(np.concatenate([fc1, fc2, b1], axis=2)),
        "b2s": a["b2s"],
        "consts": consts,
    }
    nc = bacc.Bacc("TRN2", target_bir_lowering=False, num_devices=1)
    aps = [nc.dram_tensor(k, v.shape, F32, kind="ExternalInput").ap() for k, v in arrays.items()]
    out = nc.dram_tensor("out", (B, N, D), F32, kind="ExternalOutput").ap()
    build(nc, *aps, out)
    r = run_bass_kernel_spmd(nc, [arrays], core_ids=[0])
    return r.results[0]["out"]
```

```python
import numpy as np
import concourse.bass as bass
from concourse import mybir
from contextlib import ExitStack

F32 = mybir.dt.float32
F32R = mybir.dt.float32r
BF16 = mybir.dt.bfloat16
I32 = mybir.dt.int32
U32 = mybir.dt.uint32
ALU = mybir.AluOpType
ACT = mybir.ActivationFunctionType
AX = mybir.AxisListType

P = 128
B, N, D = 16, 256, 256
H, HD = 16, 64
E, DD = 8, 1024
TOK = B * N
CAP = TOK // E
EPS = 1e-5
TT = N // P
DC = D // P
HC = DD // P
UNITS = H // 2
GU = UNITS // 2
GW = GU * 2 * HD
TILES = TOK // P
KT = CAP // P
ROW = D + E
BIG = 4096.0
BITS = 30
STEPS = BITS // 2
UPPER_STEPS = 7
UNROLLED = 4
NEWTON = 3
FIRST_LOOPED, LAST_LOOPED = 2, B - 2


CHUNKS = {(7, 0): ("q", 0), (7, 1): ("k", 0), (0, 0): ("q", 1), (0, 1): ("k", 1), (1, 0): ("v", 0), (1, 1): ("v", 1),
          (3, 0): ("q", 0), (3, 1): ("k", 0), (4, 0): ("q", 1), (4, 1): ("k", 1), (5, 0): ("v", 0), (5, 1): ("v", 1)}
ODD_STEPS = (0, 1, 7)


def group_of(b, hp):
    return b * 2 + (3 if hp == 7 else 1 if hp in ODD_STEPS else 2)


def batch_slots(b):
    cur, nxt, prv = 0 <= b < B, b + 1 < B, 1 <= b <= B
    out = [(hp, pos, name, "act") for (hp, pos), (name, _) in CHUNKS.items() if (cur if hp < 2 else nxt)]
    if prv:
        out += [(0, 2, "wout", "dve"), (6, 0, "tokT", "act"), (6, 1, "gate", "dve")]
    if nxt:
        out += [(1, 2, "xT", "act")]
    return sorted(out)


def make_counts():
    table, slots = {}, []
    totals = {}

    def hit(kind, b, key):
        totals[kind] = totals.get(kind, 0) + 1
        table[kind, b, key] = totals[kind]

    for b in range(-1, B + 1):
        cur, nxt, prv = 0 <= b < B, b + 1 < B, 1 <= b <= B
        for hp, pos, name, who in batch_slots(b):
            key = (hp, pos)
            hit("slot", b, key)
            hit(who, b, key)
            slots.append((b, key, who))
            if name in ("q", "k"):
                hit("chunk", b, key)
        for hp, live in ((0, cur or nxt), (4, nxt or prv)):
            if live:
                hit("newton", b, hp)
        for kind, live in (("x_loaded", nxt), ("xr_loaded", cur), ("tok_stored", prv)):
            if live:
                hit(kind, b, 0)
    for n, (b, key, who) in enumerate(slots):
        table["bank", b, key] = n % 2
        table["index", b, key] = n
        if n >= 2:
            pb, pkey, pwho = slots[n - 2]
            table["free", b, key] = (pwho, table[pwho, pb, pkey])
    return table


COUNTS = make_counts()


def through(kind, b, key):
    if isinstance(b, int):
        return COUNTS[kind, b, key]
    first, second = COUNTS[kind, FIRST_LOOPED, key], COUNTS[kind, FIRST_LOOPED + 1, key]
    step = second - first
    assert COUNTS[kind, LAST_LOOPED, key] == first + step * (LAST_LOOPED - FIRST_LOOPED)
    return b * step + (first - step * FIRST_LOOPED)


def bank_free(b, key):
    bi = b if isinstance(b, int) else FIRST_LOOPED + 1
    if ("free", bi, key) not in COUNTS:
        return None
    who, count = COUNTS["free", bi, key]
    if isinstance(b, int):
        return who, count
    who1, c1 = COUNTS["free", bi + 1, key]
    who0, c0 = COUNTS["free", bi - 1, key]
    assert who0 == who1 == who and c1 - count == count - c0
    return who, b * (c1 - count) + (count - (c1 - count) * bi)


def slot_bank(b, key):
    return COUNTS["bank", b if isinstance(b, int) else FIRST_LOOPED, key]


class Need:

    def __init__(self, eng):
        self.eng = eng

    def __call__(self, sem, count):
        if isinstance(count, int) and count <= 0:
            return
        self.eng.wait_ge(sem, count)


def over_batches(eng, batch):
    batch(-1, cur=False, nxt=True, prv=False)
    batch(0, cur=True, nxt=True, prv=False)
    batch(1, cur=True, nxt=True, prv=True)
    with eng.Fori(FIRST_LOOPED, LAST_LOOPED + 1) as b:
        batch(b, cur=True, nxt=True, prv=True)
    batch(B - 1, cur=True, nxt=False, prv=True)
    batch(B, cur=False, nxt=False, prv=True)


def build(nc, x, condT, w_adaT, vecs, w_qkvT, w_outT, w_gateT, experts, b2s, consts, out):
    ctx = ExitStack()
    with ctx:
        place = [ctx]

        def sb(name, shape, dt=F32):
            return place[0].enter_context(nc.sbuf_tensor(name, shape, dt))

        def ps(name, shape):
            return ctx.enter_context(nc.psum_tensor(name, shape, F32))

        def sem(name):
            return ctx.enter_context(nc.semaphore(name))

        rows_dram = nc.dram_tensor("rows_dram", [TOK, ROW], F32, kind="Internal").ap()

        NV = vecs.shape[1]
        NCON = consts.shape[1]
        vec = sb("vec", [P, NV])
        con = sb("con", [P, NCON])
        LN1_G, LN1_B, B_ADA, MLP_G, MLP_B, GQ, BQ, GK, BK = 0, 2, 4, 6, 8, 10, 11, 12, 13
        ident = con[:, 0:P]
        same_expert = con[:, P:2 * P]
        earlier_tile = con[:, 2 * P:3 * P]
        iota32 = con[:, 3 * P:3 * P + 32]
        partno = con[:, 3 * P + 32:3 * P + 33]
        tileno = iota32
        AT = 3 * P + 33
        same_low_a = con[:, AT:AT + 8]
        same_tile = con[:, AT + 8:AT + 8 + 4 * KT]
        neg_ident = sb("neg_ident", [P, P], BF16)
        same_b = sb("same_b", [P, P], BF16)

        logit = sb("logit", [P, TILES, E])

        NH = 4 * GU * 2
        tok = sb("tok", [P, TT, D])
        xh2 = sb("xh2", [P, TT, D])
        var = sb("var", [P, NH + 4])
        var_half = sb("var_half", [P, NH + 4], I32)
        ny = sb("ny", [P, NH + 4])
        na = sb("na", [P, NH + 4])
        rstd = [sb(f"rstd{i}", [P, NH + 4]) for i in range(2)]
        bn = sb("bn", [P, 4, 6])
        held_v = sb("held_v", [P, 1])
        mv = sb("mv", [P, 4, 2])

        scope = ExitStack()
        place[0] = scope
        condT_sb = sb("condT_sb", [P, DC, B])
        sig = sb("sig", [P, DC, B])
        silu = sb("silu", [P, DC, B])
        wada_sb = sb("wada_sb", [P, DC, D])
        bias1 = sb("bias1", [P, DC, B])
        w_hi = sb("w_hi", [P, DC, 3 * H * HD], F32R)
        w_lo = sb("w_lo", [P, DC, 3 * H * HD], F32R)
        wo_sb = sb("wo_sb", [P, UNITS, D])
        wo_hi = sb("wo_hi", [P, UNITS, D], F32R)
        wo_lo = sb("wo_lo", [P, UNITS, D], F32R)
        wg_sb = sb("wg_sb", [P, DC, E])

        x_sb = sb("x_sb", [P, TT, D])
        xr_sb = sb("xr_sb", [P, TT, D])
        xh = sb("xh", [P, TT, D])
        hT = sb("hT", [P, DC, N])
        hT_hi = sb("hT_hi", [P, DC, N], F32R)
        hT_lo = sb("hT_lo", [P, DC, N], F32R)
        w_means = sb("w_means", [P, 4, 4 * GU])
        raw = sb("raw", [P, 4, GW])
        sq = [sb(f"sq{i}", [P, GW]) for i in range(2)]
        qn = [sb(f"qn{i}", [P, 4, GW]) for i in range(2)]
        ssum = sb("ssum", [P, NH])
        held_p = sb("held_p", [P, 4])
        V = [sb(f"V{i}", [P, TT, GW]) for i in range(2)]
        ones = sb("ones", [P, HD])
        q_hi = [sb(f"q_hi{i}", [P, 2, N], F32R) for i in range(2)]
        q_lo = [sb(f"q_lo{i}", [P, 2, N], F32R) for i in range(2)]
        k_hi = [sb(f"k_hi{i}", [P, N], F32R) for i in range(2)]
        k_lo = [sb(f"k_lo{i}", [P, N], F32R) for i in range(2)]
        qkT = [sb(f"qkT{i}", [P, 2 * N]) for i in range(2)]
        m = [sb(f"m{i}", [P, 4], BF16) for i in range(2)]
        prob = [sb(f"prob{i}", [P, 2 * TT * N]) for i in range(2)]
        prob_sum = [sb(f"prob_sum{i}", [P, 2, N]) for i in range(2)]
        rec = sb("rec", [P, N])
        oT = [sb(f"oT{i}", [P, N]) for i in range(2)]
        o_hi = sb("o_hi", [P, UNITS, N], F32R)
        o_lo = sb("o_lo", [P, UNITS, N], F32R)
        tokT = sb("tokT", [P, DC, N])
        scope.close()
        place[0] = ctx

        NP = 2 * P
        top = sb("top", [P, TILES])
        gates = sb("gates", [P, TILES, E])
        gT_ = sb("gates_T", [P, 2, P])
        hit = sb("hit", [P, 3, NP], BF16)
        gates_upper = sb("gates_upper", [P, NP], BF16)
        bits = sb("bits", [P, 3], I32)
        trial = sb("trial", [P, 3], I32)
        kept = sb("kept", [P, 4])
        cnt = sb("cnt", [P, 3], BF16)
        above = sb("above", [P, 2, P])
        equal = sb("equal", [P, 2, P])
        n4 = sb("n4", [P, 4])
        d4 = sb("d4", [P, 4])
        first4 = sb("first4", [P, 4])
        zeros = sb("zeros", [P, P])
        rank_a = sb("rank_a", [P, 2, P])
        rank_e = sb("rank_e", [P, 2, P])
        rank = sb("rank", [P, 2, P])
        rank_i = sb("rank_i", [P, TILES * E], I32)
        rank_hi = sb("rank_hi", [P, TILES * E], I32)
        rank_lo = sb("rank_lo", [P, TILES * E], I32)
        RA, RB = 32, 16
        AK = P // RB
        index_a = sb("index_a", [P, 2, RB])
        spread_a = sb("spread_a", [P, 2, AK, RB])
        index = sb("index", [P, E * KT], I32)
        W1, W2 = DC * DD, HC * D
        fcw = [sb(f"fcw{i}", [P, W1 + W2]) for i in range(2)]
        b1_sb = sb("b1_sb", [P, E, HC])
        w1_hi = sb("w1_hi", [P, DC, DD], F32R)
        w1_lo = sb("w1_lo", [P, DC, DD], F32R)
        w2_hi = [sb(f"w2_hi{i}", [P, HC, D], F32R) for i in range(2)]
        w2_lo = [sb(f"w2_lo{i}", [P, HC, D], F32R) for i in range(2)]
        b2_sb = sb("b2_sb", [P, E, D])
        got = [sb(f"got{i}", [P, KT, ROW]) for i in range(2)]
        gT = sb("gT", [P, DC, CAP])
        gT_hi = sb("gT_hi", [P, DC, CAP], F32R)
        gT_lo = sb("gT_lo", [P, DC, CAP], F32R)
        yT = sb("yT", [P, 2, CAP])
        scope = ExitStack()
        place[0] = scope
        rank_hi_b = sb("rank_hi_b", [P, TILES * E], BF16)
        rank_lo_b = sb("rank_lo_b", [P, TILES * E], BF16)
        tile_b = sb("tile_b", [P, TILES * E], BF16)
        one_a = sb("one_a", [P, RA, TILES * E], BF16)
        one_b = sb("one_b", [P, RB, TILES * E], BF16)
        val_b = sb("val_b", [P, 2, RB, TILES * E], BF16)
        parts = sb("parts", [P, 2, RB])
        scope.close()
        place[0] = ctx
        yT_hi = sb("yT_hi", [P, HC, CAP], F32R)
        yT_lo = sb("yT_lo", [P, HC, CAP], F32R)
        ysum = sb("ysum", [P, 2, D])
        yout = [sb(f"yout{i}", [P, KT, D]) for i in range(2)]

        pq = ps("pq", [P, 512])
        ch = [ps(f"ch{i}", [P, 512]) for i in range(2)]
        mx = ps("mx", [P, 1024])
        sc = ps("sc", [P, 1024])
        av = ps("av", [P, 512])

        con_in = sem("con_in")
        cond_in = sem("cond_in")
        wqk_in = [[sem(f"wqk_in{g}{c}") for c in range(DC)] for g in range(2)]
        wv_in = sem("wv_in")
        wsmall_in = sem("wsmall_in")
        x_in = sem("x_in")
        xr_in = sem("xr_in")
        tok_out = sem("tok_out")
        row_out = sem("row_out")
        consts_ready = sem("consts_ready")
        tanh_done = sem("tanh_done")
        silu_ready = sem("silu_ready")
        shift_done = sem("shift_done")
        bias1_ready = sem("bias1_ready")
        w_centred = sem("w_centred")
        wqk_hi_ready = sem("wqk_hi_ready")
        wv_hi_ready = sem("wv_hi_ready")
        w_lo_first_ready = sem("w_lo_first_ready")
        w_lo_rest_ready = sem("w_lo_rest_ready")
        pads_ready = sem("pads_ready")
        qk_transposed = sem("qk_transposed")
        qk_evacuated = sem("qk_evacuated")
        hi_ready = sem("hi_ready")
        pre_scored = sem("pre_scored")
        max_ready = sem("max_ready")
        scored = sem("scored")
        prob_ready = sem("prob_ready")
        attended = sem("attended")
        normed = sem("normed")
        divided = sem("divided")
        qn_pool_ready = sem("qn_pool_ready")
        lo_ready = sem("lo_ready")
        k_split = sem("k_split")
        prob_summed = sem("prob_summed")
        o_split = sem("o_split")
        wo_ready = sem("wo_ready")
        slot_filled = sem("slot_filled")
        act_read = sem("act_read")
        dve_read = sem("dve_read")
        chunk_summed = sem("chunk_summed")
        rstd_ready = sem("rstd_ready")
        hT_split = sem("hT_split")
        qn_ready = sem("qn_ready")
        xh_ready = sem("xh_ready")
        xh2_ready = sem("xh2_ready")
        dve_step = sem("dve_step")
        free_sem = {"act": act_read, "dve": dve_read}

        class Chain:

            def __init__(self, eng, semaphore, base=0):
                self.eng, self.sem, self.base, self.n = eng, semaphore, base, 0

            def count(self):
                return self.base + self.n

            def base_loop(self, base):
                self.kept, self.base = self.base, self.base + base

            def base_end(self, base):
                self.base = self.kept + base

            def __call__(self, ins):
                self.n += 1
                ins.then_inc(self.sem, 1)
                self.eng.wait_ge(self.sem, self.count())

        logits_ready = sem("logits_ready")
        exp_done = sem("exp_done")
        gates_ready = sem("gates_ready")
        gates_out = sem("gates_out")
        gates_transposed = sem("gates_transposed")
        counted_ready = sem("counted_ready")
        totals_ready = sem("totals_ready")
        n4_ready = sem("n4_ready")
        firsts_ready = sem("firsts_ready")
        rank_ready = sem("rank_ready")
        rank_transposed = sem("rank_transposed")
        hot_ready = sem("hot_ready")
        lists_ready = sem("lists_ready")
        index_a_ready = sem("index_a_ready")
        lists_spread = sem("lists_spread")
        index_ready = sem("index_ready")
        b2_in = sem("b2_in")
        fc_in = [sem(f"fc_in{i}") for i in range(2)]
        gathered = [sem(f"gathered{i}") for i in range(2)]
        scattered = sem("scattered")
        g_transposed = sem("g_transposed")
        gT_ready = sem("gT_ready")
        b1_in = sem("b1_in")
        gT_lo_ready = sem("gT_lo_ready")
        w1_hi_ready = sem("w1_hi_ready")
        first_w1_lo_ready = sem("first_w1_lo_ready")
        first_w2_lo_ready = sem("first_w2_lo_ready")
        w1_lo_ready = sem("w1_lo_ready")
        w2_hi_ready = sem("w2_hi_ready")
        w2_lo_ready = sem("w2_lo_ready")
        y_split = sem("y_split")
        y_hi_ready = sem("y_hi_ready")
        fc1_done = sem("fc1_done")
        gelu_done = sem("gelu_done")
        fc2_done = sem("fc2_done")
        fc2_read = sem("fc2_read")
        y_ready = sem("y_ready")

        block = ctx.enter_context(nc.Block())

        def raw_qk(g, c):
            return (prob[g][:, :] if c == 0 else qn[1][:, 2 * g:2 * g + 2, :].rearrange("p a n -> p (a n)")).rearrange("p (a n) -> p a n", a=2)

        def raw_v(c):
            return V[c][:, :, :].rearrange("p t n -> p (t n)")

        def split_qk(w, g, c):
            return w[:, c, 0:2 * H * HD].rearrange("p (a g n) -> p g a n", a=2, g=2)[:, g, :, :]

        def three_passes(psum, l_hi, l_lo, r_hi, r_lo, first, last):
            nc.tensor.matmul(psum, l_lo, r_hi, start=first, stop=False)
            nc.tensor.matmul(psum, l_hi, r_lo, start=False, stop=False)
            return nc.tensor.matmul(psum, l_hi, r_hi, start=False, stop=last)

        fc2_bank = (sc[:, 0:D], sc[:, 512:512 + D], av[:, 0:D], pq[:, 0:D])

        def over_experts(eng, expert):
            expert(0, 0, 0)
            expert(1, 0, 1)
            with eng.Fori(1, E // 2 - 1) as i:
                expert(i * 2, i, 0)
                expert(i * 2 + 1, i, 1)
            expert(E - 2, E // 2 - 1, 0)
            expert(E - 1, E // 2 - 1, 1)

        def w_lo_wait(eng, layer, e):
            if isinstance(e, int) and e == 0:
                eng.wait_ge((first_w1_lo_ready, first_w2_lo_ready)[layer - 1], 1)
            else:
                eng.wait_ge((w1_lo_ready, w2_lo_ready)[layer - 1], e)

        def is_last(e):
            return isinstance(e, int) and e == E - 1

        def next_pair(pair, par):
            return pair + 1 if par else pair

        def raw_w(par):
            return fcw[par][:, 0:W1], fcw[par][:, W1:W1 + W2]

        def flat(t):
            return t[:, :, :].rearrange("p a n -> p (a n)")

        def store_rows(sp, b):
            Need(sp)(xh2_ready, b)
            r = (rows_dram[bass.ds((b - 1) * N, N)] if not isinstance(b, int)
                 else rows_dram[(b - 1) * N:b * N])
            sp.dma_start(r[:, 0:D].rearrange("(t p) d -> p t d", p=P), xh2[:, :, :]).then_inc(row_out, 16)

        def phase23_sync(sp):
            need = Need(sp)
            sp.wait_ge(logits_ready, 1)
            sp.dma_start(b2_sb[:, :, :].rearrange("p e d -> p (e d)"),
                         b2s.rearrange("(o e) d -> o (e d)", o=1).to_broadcast([P, E * D])).then_inc(b2_in, 16)

            def load(e, par):
                src = experts[e] if isinstance(e, int) else experts[bass.ds(e, 1)].rearrange("o p n -> p (o n)")
                sp.dma_start(fcw[par][:, :], src[:, 0:W1 + W2]).then_inc(fc_in[par], 16)

            load(0, 0)
            load(1, 1)
            sp.dma_start(b1_sb[:, :, :], experts[:, :, W1 + W2:W1 + W2 + HC].rearrange("e p n -> p e n")).then_inc(b1_in, 16)
            sp.wait_ge(gates_ready, 1)
            sp.dma_start(rows_dram[:, D:ROW].rearrange("(t p) e -> p t e", p=P), gates[:, :, :]).then_inc(gates_out, 16)
            store_rows(sp, B)
            def expert(e, par):
                w_lo_wait(sp, 2, e)
                load(e + 2, par)
            expert(0, 0)
            expert(1, 1)
            with sp.Fori(1, E // 2 - 1) as i:
                expert(i * 2, 0)
                expert(i * 2 + 1, 1)

        def phase23_pool(pool):
            w1, w2 = raw_w(0)
            pool.wait_ge(w1_hi_ready, 1)
            nc.gpsimd.tensor_tensor(flat(w1_lo), w1, flat(w1_hi).bitcast(F32), ALU.subtract).then_inc(first_w1_lo_ready, 1)
            pool.wait_ge(w2_hi_ready, 1)
            nc.gpsimd.tensor_tensor(flat(w2_lo[0]), w2, flat(w2_hi[0]).bitcast(F32), ALU.subtract).then_inc(first_w2_lo_ready, 1)
            pool.wait_ge(index_ready, 1)
            pool.wait_ge(gates_out, 16)
            pool.wait_ge(row_out, B * 16)
            pool.wait_ge(tok_out, B * 16)

            def gather(e):
                par = e % 2
                if e >= 2:
                    pool.wait_ge(y_ready, (e - 1) * KT)
                for k in range(KT):
                    nc.gpsimd.indirect_dma_start(
                        out=got[par][:, k, :], out_offset=None, in_=rows_dram,
                        in_offset=bass.IndirectOffsetOnAxis(ap=index[:, e * KT + k:e * KT + k + 1].bitcast(U32), axis=0),
                        compute_op=ALU.bypass).then_inc(gathered[par], 16)

            gather(0)
            gather(1)
            for e in range(E):
                if e >= 1:
                    pool.wait_ge(scattered, 16 * KT * e)
                for k in range(KT):
                    pool.wait_ge(y_ready, e * KT + k + 1)
                    nc.gpsimd.indirect_dma_start(
                        out=out.rearrange("b n d -> (b n) d"),
                        out_offset=bass.IndirectOffsetOnAxis(ap=index[:, e * KT + k:e * KT + k + 1].bitcast(U32), axis=0),
                        in_=yout[e % 2][:, k, :], in_offset=None,
                        compute_op=ALU.add).then_inc(scattered, 16)
                if e + 2 < E:
                    gather(e + 2)
            pool.wait_ge(scattered, 16 * KT * E)

        def phase23_scalar(act):
            act.wait_ge(logits_ready, 1)
            nc.scalar.activation(gates[:, :, :], gates[:, :, :], ACT.Exp).then_inc(exp_done, 1)

            def split_w1(pair, par):
                act.wait_ge(fc_in[par], (pair + 1) * 16)
                nc.scalar.activation(flat(w1_hi), raw_w(par)[0], ACT.Copy).then_inc(w1_hi_ready, 1)

            def split_w2(par):
                nc.scalar.activation(flat(w2_hi[par]), raw_w(par)[1], ACT.Copy).then_inc(w2_hi_ready, 1)

            def tokens(e):
                act.wait_ge(g_transposed, e + 1)
                if not (isinstance(e, int) and e == 0):
                    act.wait_ge(gT_lo_ready, e)
                for dst in (gT_hi, gT):
                    for c in range(DC):
                        ins = nc.scalar.activation(dst[:, c, :], mx[:, c * CAP:(c + 1) * CAP], ACT.Identity,
                                                   bias=vec[:, MLP_B + c:MLP_B + c + 1], scale=vec[:, MLP_G + c:MLP_G + c + 1])
                ins.then_inc(gT_ready, 1)

            split_w1(0, 0)
            split_w2(0)
            tokens(0)
            act.wait_ge(b1_in, 16)

            def expert(e, pair, par):
                for hc in range(HC):
                    act.wait_ge(fc1_done, e * HC + hc + 1)
                    if not (isinstance(e, int) and e == 0 and hc < 2):
                        act.wait_ge(y_split, e * HC + hc - 1)
                    b1 = (b1_sb[:, e, hc:hc + 1] if isinstance(e, int) else flat(b1_sb)[:, bass.ds(e * HC + hc, 1)])
                    nc.scalar.activation(yT[:, hc % 2, :], ch[hc % 2][:, :], ACT.Gelu_apprx_tanh, bias=b1).then_inc(gelu_done, 1)
                if not is_last(e):
                    split_w1(next_pair(pair, par), 1 - par)
                    tokens(e + 1)
                    split_w2(1 - par)
            over_experts(act, expert)

        def phase23_tensor(pe):
            pe.wait_ge(gates_ready, 1)
            for blk in range(2):
                ins = nc.tensor.transpose(mx[:, blk * P:(blk + 1) * P],
                                          gates[:, blk * 16:(blk + 1) * 16, :].rearrange("p t e -> p (t e)"), ident)
            ins.then_inc(gates_transposed, 1)
            def totals(step):
                pe.wait_ge(counted_ready, step)
                nc.tensor.matmul(av[:, 0:3], same_b[:, :], cnt[:, :], start=True, stop=True).then_inc(totals_ready, 1)
            for step in range(UPPER_STEPS):
                totals(step + 1)
            with pe.Fori(0, (STEPS - UPPER_STEPS) // UNROLLED) as i:
                for step in range(UNROLLED):
                    totals(i * UNROLLED + (UPPER_STEPS + step + 1))
            pe.wait_ge(n4_ready, 1)
            nc.tensor.matmul(av[:, 4:8], earlier_tile, n4[:, :], start=True, stop=False)
            nc.tensor.matmul(av[:, 4:8], same_expert, d4[:, :], start=False, stop=True).then_inc(firsts_ready, 1)
            pe.wait_ge(rank_ready, 1)
            for blk in range(2):
                ins = nc.tensor.transpose(mx[:, 512 + blk * P:512 + (blk + 1) * P], rank[:, blk, :], ident)
            ins.then_inc(rank_transposed, 1)
            pe.wait_ge(hot_ready, 1)
            for e in range(E):
                q = 32 * (e % 4)
                for t in range(TILES):
                    c = t * E + e
                    ins = nc.tensor.matmul(ch[e // 4][q:q + RA, 0:2 * RB], one_a[:, :, c], val_b[:, :, :, c].rearrange("p v b -> p (v b)"),
                                           start=(t == 0), stop=(t == TILES - 1))
            ins.then_inc(lists_ready, 1)

            pe.wait_ge(index_a_ready, 1)
            for h in range(2):
                ins = nc.tensor.matmul(pq[:, h * 4 * KT:(h + 1) * 4 * KT], spread_a[:, h, :, :].rearrange("p a b -> p (a b)"), same_tile,
                                       start=True, stop=True)
            ins.then_inc(lists_spread, 1)
            pe.wait_ge(gathered[0], 16 * KT)
            for c in range(DC):
                for k in range(KT):
                    ins = nc.tensor.transpose(mx[:, c * CAP + k * P:c * CAP + (k + 1) * P], got[0][:, k, c * P:(c + 1) * P], ident)
            ins.then_inc(g_transposed, 1)

            def expert(e, pair, par):
                pe.wait_ge(w1_hi_ready, e + 1)
                w_lo_wait(pe, 1, e)
                pe.wait_ge(gT_ready, e + 1)
                pe.wait_ge(gT_lo_ready, e + 1)
                for hc in range(HC):
                    if not (isinstance(e, int) and e == 0 and hc < 2):
                        pe.wait_ge(gelu_done, e * HC + hc - 1)
                    for c in range(DC):
                        cols = slice(hc * P, (hc + 1) * P)
                        ins = three_passes(ch[hc % 2][:, :], w1_hi[:, c, cols], w1_lo[:, c, cols], gT_hi[:, c, :], gT_lo[:, c, :],
                                           c == 0, c == DC - 1)
                    ins.then_inc(fc1_done, 1)
                if not is_last(e):
                    pe.wait_ge(gathered[1 - par], (next_pair(pair, par) + 1) * (16 * KT))
                    for c in range(DC):
                        for k in range(KT):
                            ins = nc.tensor.transpose(mx[:, c * CAP + k * P:c * CAP + (k + 1) * P], got[1 - par][:, k, c * P:(c + 1) * P], ident)
                    ins.then_inc(g_transposed, 1)
                pe.wait_ge(w2_hi_ready, e + 1)
                w_lo_wait(pe, 2, e)
                for k in range(KT):
                    if not (isinstance(e, int) and e == 0):
                        pe.wait_ge(fc2_read, (e - 1) * KT + k + 1)
                    for hc in range(HC):
                        if k == 0:
                            pe.wait_ge(y_split, e * HC + hc + 1)
                        rows = slice(k * P, (k + 1) * P)
                        ins = three_passes(fc2_bank[k], yT_hi[:, hc, rows], yT_lo[:, hc, rows], w2_hi[par][:, hc, :], w2_lo[par][:, hc, :],
                                           hc == 0, hc == HC - 1)
                    ins.then_inc(fc2_done, 1)

            over_experts(pe, expert)

        def phase23_vector(dve, chain, last_rows):
            V_ = nc.vector
            thr_i = kept[:, 3:4].bitcast(I32)
            dve.wait_ge(dve_read, 2 * B)
            chain(V_.tensor_reduce(top[:, :], logit[:, :, :], AX.X, ALU.max))
            top3 = top[:, :].rearrange("p (t o) -> p t o", o=1).to_broadcast([P, TILES, E])
            V_.tensor_tensor(gates[:, :, :], logit[:, :, :], top3, ALU.subtract).then_inc(logits_ready, 1)
            dve.wait_ge(exp_done, 1)
            chain(V_.tensor_reduce(top[:, :], gates[:, :, :], AX.X, ALU.add))
            chain(V_.reciprocal(top[:, :], top[:, :]))
            V_.tensor_tensor(gates[:, :, :], gates[:, :, :], top3, ALU.mult).then_inc(gates_ready, 1)
            V_.memset(zeros[:, :], 0.0)
            V_.tensor_copy(tile_b[:, :].rearrange("p (t e) -> p t e", e=E),
                           tileno.rearrange("p (t o) -> p t o", o=1).to_broadcast([P, TILES, E]))
            V_.memset(d4[:, :], 0.0)
            for k in range(3):
                V_.memset(bits[:, k:k + 1], (k + 1) << (BITS - 2))
            chain(V_.memset(thr_i, 0))
            dve.wait_ge(gates_transposed, 1)
            chain(V_.tensor_copy(gT_[:, :, :].rearrange("p b t -> p (b t)"), mx[:, 0:NP]))
            chain(V_.tensor_copy(gates_upper[:, :], gT_[:, :, :].rearrange("p b t -> p (b t)").bitcast(BF16)[:, 1::2]))
            def search_step(of, totals):
                chain(V_.tensor_tensor(trial[:, :], bits[:, :], thr_i.to_broadcast([P, 3]), ALU.bitwise_or))
                for k in range(3):
                    ins = V_.tensor_scalar(hit[:, k, :], of, trial[:, k:k + 1].bitcast(F32), 0.0, ALU.is_ge, ALU.add, accum_out=cnt[:, k:k + 1])
                ins.then_inc(counted_ready, 1)
                chain(V_.tensor_scalar(bits[:, :], bits[:, :], 2, None, ALU.logical_shift_right))
                dve.wait_ge(totals_ready, totals)
                chain(V_.scalar_tensor_tensor(kept[:, 0:3], av[:, 0:3], CAP - 0.5, trial[:, :].bitcast(F32), ALU.is_ge, ALU.mult))
                chain(V_.tensor_reduce(kept[:, 3:4], kept[:, :], AX.X, ALU.max))
            for step in range(UPPER_STEPS):
                search_step(gates_upper[:, :], step + 1)
            before = chain.n
            with dve.Fori(0, (STEPS - UPPER_STEPS) // UNROLLED) as i:
                chain.base_loop(i * (4 * UNROLLED))
                for step in range(UNROLLED):
                    search_step(gT_[:, :, :].rearrange("p b t -> p (b t)"), i * UNROLLED + (UPPER_STEPS + step + 1))
            assert chain.n - before == 4 * UNROLLED
            chain.base_end(4 * UNROLLED * ((STEPS - UPPER_STEPS) // UNROLLED - 1))
            t_ = kept[:, 3:4]
            V_.tensor_scalar(above[:, :, :], gT_[:, :, :], t_, None, ALU.is_gt)
            chain(V_.tensor_scalar(equal[:, :, :], gT_[:, :, :], t_, None, ALU.is_equal))
            V_.tensor_reduce(n4[:, 0:2], above[:, :, :], AX.X, ALU.add)
            chain(V_.tensor_reduce(n4[:, 2:4], equal[:, :, :], AX.X, ALU.add))
            for i in range(3):
                ins = V_.tensor_tensor(d4[:, i + 1:i + 2], d4[:, i:i + 1], n4[:, i:i + 1], ALU.add)
                if i < 2:
                    chain(ins)
            ins.then_inc(n4_ready, 1)
            dve.wait_ge(firsts_ready, 1)
            chain(V_.tensor_scalar(first4[:, :], av[:, 4:8], -1.0, None, ALU.add))
            for blk in range(2):
                V_.tensor_tensor_scan(rank_a[:, blk, :], above[:, blk, :], zeros[:, :], first4[:, blk:blk + 1], ALU.add, ALU.add)
                ins = V_.tensor_tensor_scan(rank_e[:, blk, :], equal[:, blk, :], zeros[:, :], first4[:, 2 + blk:3 + blk], ALU.add, ALU.add)
            chain(ins)
            V_.tensor_tensor(rank_a[:, :, :], rank_a[:, :, :], above[:, :, :], ALU.mult)
            chain(V_.tensor_tensor(rank_e[:, :, :], rank_e[:, :, :], equal[:, :, :], ALU.mult))
            V_.tensor_tensor(rank_a[:, :, :], rank_a[:, :, :], rank_e[:, :, :], ALU.add)
            chain(V_.tensor_tensor(above[:, :, :], above[:, :, :], equal[:, :, :], ALU.add))
            chain(V_.tensor_scalar(above[:, :, :], above[:, :, :], -BIG, BIG, ALU.mult, ALU.add))
            V_.tensor_tensor(rank[:, :, :], rank_a[:, :, :], above[:, :, :], ALU.add).then_inc(rank_ready, 1)
            dve.wait_ge(rank_transposed, 1)
            chain(V_.tensor_copy(rank_i[:, :], mx[:, 512:512 + NP]))
            V_.tensor_scalar(rank_hi[:, :], rank_i[:, :], 4, None, ALU.logical_shift_right)
            chain(V_.tensor_scalar(rank_lo[:, :], rank_i[:, :], RB - 1, None, ALU.bitwise_and))
            V_.tensor_copy(rank_hi_b[:, :], rank_hi[:, :])
            chain(V_.tensor_copy(rank_lo_b[:, :], rank_lo[:, :]))
            for b in range(RB):
                ins = V_.tensor_scalar(one_b[:, b, :], rank_lo_b[:, :], float(b), None, ALU.is_equal)
            chain(ins)
            V_.tensor_scalar(val_b[:, 0, :, :], one_b[:, :, :], partno, None, ALU.mult)
            V_.tensor_tensor(val_b[:, 1, :, :], one_b[:, :, :],
                             tile_b[:, :].rearrange("p (o n) -> p o n", o=1).to_broadcast([P, RB, TILES * E]), ALU.mult)
            for a in range(RA):
                ins = V_.tensor_scalar(one_a[:, a, :], rank_hi_b[:, :], float(a), None, ALU.is_equal)
            ins.then_inc(hot_ready, 1)
            last_rows()
            dve.wait_ge(lists_ready, 1)
            for h in range(2):
                ins = V_.tensor_copy(parts[:, h, :], ch[h][:, RB:2 * RB])
            chain(ins)
            for h in range(2):
                ins = V_.scalar_tensor_tensor(index_a[:, h, :], parts[:, h, :], float(P), ch[h][:, 0:RB], ALU.mult, ALU.add)
            chain(ins)
            for h in range(2):
                ins = V_.tensor_tensor(spread_a[:, h, :, :], index_a[:, h, :].rearrange("p (o b) -> p o b", o=1).to_broadcast([P, AK, RB]),
                                       same_low_a.rearrange("p (a o) -> p a o", o=1).to_broadcast([P, AK, RB]), ALU.mult)
            ins.then_inc(index_a_ready, 1)
            dve.wait_ge(lists_spread, 1)
            V_.tensor_copy(index[:, :], pq[:, 0:E * KT]).then_inc(index_ready, 1)

            dve.wait_ge(b2_in, 16)

            def low_part(lo, full, hi, ready):
                V_.tensor_tensor(lo, full, hi.bitcast(F32), ALU.subtract).then_inc(ready, 1)

            dve.wait_ge(gT_ready, 1)
            low_part(flat(gT_lo), flat(gT), flat(gT_hi), gT_lo_ready)

            def expert(e, pair, par):
                for hc in range(HC):
                    dve.wait_ge(gelu_done, e * HC + hc + 1)
                    V_.tensor_copy(yT_hi[:, hc, :], yT[:, hc % 2, :]).then_inc(y_hi_ready, 1)
                    dve.wait_ge(y_hi_ready, e * HC + hc + 1)
                    low_part(yT_lo[:, hc, :], yT[:, hc % 2, :], yT_hi[:, hc, :], y_split)
                if not is_last(e):
                    w1, w2 = raw_w(1 - par)
                    dve.wait_ge(w1_hi_ready, e + 2)
                    low_part(flat(w1_lo), w1, flat(w1_hi), w1_lo_ready)
                    dve.wait_ge(gT_ready, e + 2)
                    low_part(flat(gT_lo), flat(gT), flat(gT_hi), gT_lo_ready)
                    dve.wait_ge(w2_hi_ready, e + 2)
                    low_part(flat(w2_lo[1 - par]), w2, flat(w2_hi[1 - par]), w2_lo_ready)
                for k in range(KT):
                    dve.wait_ge(fc2_done, e * KT + k + 1)
                    if k == 0 and not (isinstance(e, int) and e < 2):
                        dve.wait_ge(scattered, (e - 1) * (16 * KT))
                    b2 = b2_sb[:, e, :] if isinstance(e, int) else flat(b2_sb)[:, bass.ds(e * D, D)]
                    w = (got[par][:, k, D + e:D + e + 1] if isinstance(e, int) else got[par][:, k, bass.ds(e + D, 1)])
                    V_.tensor_tensor(ysum[:, k % 2, :], fc2_bank[k], b2, ALU.add).then_inc(fc2_read, 1)
                    dve.wait_ge(fc2_read, e * KT + k + 1)
                    V_.tensor_scalar(yout[par][:, k, :], ysum[:, k % 2, :], w, None, ALU.mult).then_inc(y_ready, 1)
            over_experts(dve, expert)

        POOL_CHUNKS = 1

        def times_rstd(eng, par, c):
            r = rstd[par][:, c * 8:(c + 1) * 8].rearrange("p (h o) -> p h o", o=1).to_broadcast([P, 8, HD])
            return eng.tensor_tensor(qn[par][:, c, :].rearrange("p (h d) -> p h d", d=HD),
                                     raw[:, c, :].rearrange("p (h d) -> p h d", d=HD), r, ALU.mult)

        def sync_batch(sp):
            need = Need(sp)

            def batch(b, cur, nxt, prv):
                if nxt and not (isinstance(b, int) and b < 0):
                    need(xh_ready, b + 1)
                    sp.dma_start(x_sb[:, :, :], x[bass.ds(b + 1, 1)].rearrange("o (t p) d -> p (o t) d", p=P)
                                 if not isinstance(b, int) else x[b + 1].rearrange("(t p) d -> p t d", p=P)).then_inc(x_in, 16)
                if prv:
                    need(dve_read, through("dve", b, (0, 2)))
                    dst = (out[bass.ds(b - 1, 1)].rearrange("o (t p) d -> p (o t) d", p=P)
                           if not isinstance(b, int) else out[b - 1].rearrange("(t p) d -> p t d", p=P))
                    sp.dma_start(dst, tok[:, :, :]).then_inc(tok_out, 16)
                if cur:
                    src = (x[bass.ds(b, 1)].rearrange("o (t p) d -> p (o t) d", p=P)
                           if not isinstance(b, int) else x[b].rearrange("(t p) d -> p t d", p=P))
                    sp.dma_start(xr_sb[:, :, :], src).then_inc(xr_in, 16)
                if prv and not (isinstance(b, int) and b == B):
                    store_rows(sp, b)
            return batch

        @block.sync
        def _(sp):
            sp.dma_start(x_sb[:, :, :], x[0].rearrange("(t p) d -> p t d", p=P)).then_inc(x_in, 16)
            sp.dma_start(con[:, :], consts).then_inc(con_in, 16)
            sp.dma_start(condT_sb[:, :, :], condT).then_inc(cond_in, 16)
            sp.dma_start(wada_sb[:, :, :], w_adaT).then_inc(cond_in, 16)
            sp.dma_start(vec[:, :], vecs).then_inc(cond_in, 16)
            for g in range(2):
                for c in range(DC):
                    src = w_qkvT[:, c, 0:2 * H * HD].rearrange("p (a g n) -> p g a n", a=2, g=2)[:, g, :, :]
                    sp.dma_start(raw_qk(g, c), src).then_inc(wqk_in[g][c], 16)
                if g == 0:
                    for c in range(DC):
                        sp.dma_start(raw_v(c), w_qkvT[:, c, 2 * H * HD:3 * H * HD]).then_inc(wv_in, 16)
            sp.dma_start(wo_sb[:, :, :], w_outT).then_inc(wsmall_in, 16)
            sp.dma_start(wg_sb[:, :, :], w_gateT).then_inc(wsmall_in, 16)
            over_batches(sp, sync_batch(sp))
            phase23_sync(sp)

        @block.gpsimd
        def _(pool):
            need = Need(pool)
            for i in range(2):
                nc.gpsimd.memset(q_hi[i][:, :, :].bitcast(F32), 0.0).then_inc(pads_ready, 1)
                nc.gpsimd.memset(q_lo[i][:, :, :].bitcast(F32), 0.0).then_inc(pads_ready, 1)
            nc.gpsimd.memset(ones[:, :], 1.0).then_inc(pads_ready, 1)
            for c in range(DC):
                pool.wait_ge(wv_hi_ready, c + 1)
                ins = nc.gpsimd.tensor_tensor(w_lo[:, c, 2 * H * HD:], raw_v(c), w_hi[:, c, 2 * H * HD:].bitcast(F32), ALU.subtract)
                ins.then_inc(w_lo_rest_ready, 1)
            for c in range(DC):
                pool.wait_ge(wqk_hi_ready, DC + c + 1)
                nc.gpsimd.tensor_tensor(split_qk(w_lo, 1, c), raw_qk(1, c), split_qk(w_hi, 1, c).bitcast(F32),
                                        ALU.subtract).then_inc(w_lo_rest_ready, 1)

            def split_wout(pair):
                pool.wait_ge(wsmall_in, 32)
                nc.gpsimd.tensor_copy(wo_hi[:, pair, :], wo_sb[:, pair, :]).then_inc(wo_ready, 1)
                pool.wait_ge(wo_ready, 2 * pair + 1)
                nc.gpsimd.tensor_tensor(wo_lo[:, pair, :], wo_sb[:, pair, :], wo_hi[:, pair, :].bitcast(F32), ALU.subtract).then_inc(wo_ready, 1)

            def batch(b, cur, nxt, prv):
                def normalise(hp, c):
                    par = 1 if hp == 0 else 0
                    g = b * 2 + (1 if hp == 0 else 2)
                    if c == 0:
                        need(rstd_ready, through("newton", b, hp))
                        need(qk_transposed, (g - 1) * GU)
                    ins = times_rstd(nc.gpsimd, par, c)
                    if c == POOL_CHUNKS - 1:
                        ins.then_inc(qn_pool_ready, 1)

                for hp in range(UNITS):
                    u = b * UNITS + hp
                    par = (hp + 1) % 2
                    if (cur and hp > 0) or (hp == 0 and prv):
                        need(prob_ready, u)
                        need(attended, u - 2)
                        pr = prob[(hp - 1) % 2][:, :].rearrange("p (h t n) -> p h t n", h=2, t=TT)
                        nc.gpsimd.tensor_tensor(prob_sum[(hp - 1) % 2][:, :, :], pr[:, :, 0, :], pr[:, :, 1, :], ALU.add).then_inc(prob_summed, 1)
                    if (cur and nxt) or (cur and hp < UNITS - 1) or (nxt and hp == UNITS - 1):
                        need(qk_evacuated, u + 2)
                        need(scored, u)
                        f, lo, hi = qkT[par], q_lo[par], q_hi[par]
                        nc.gpsimd.tensor_tensor(k_lo[par][:, :], f[:, N:2 * N], k_hi[par][:, :].bitcast(F32), ALU.subtract).then_inc(k_split, 1)
                        nc.gpsimd.tensor_tensor(lo[0:64, 0, :], f[0:64, 0:N], hi[0:64, 0, :].bitcast(F32), ALU.subtract)
                        need(k_split, u + 2)
                        nc.gpsimd.tensor_tensor(lo[64:128, 1, :], f[64:128, 0:N], hi[64:128, 1, :].bitcast(F32), ALU.subtract).then_inc(lo_ready, 1)
                        need(lo_ready, u + 2)
                        nc.gpsimd.tensor_tensor(held_p[:, 3:4], partno, partno, ALU.add)
                    if (cur and hp > 1) or (hp == 0 and prv):
                        for pair in ((hp - 2,) if hp else (UNITS - 2, UNITS - 1)):
                            need(normed, u - 1 if pair != UNITS - 1 else u)
                            nc.gpsimd.tensor_tensor(o_lo[:, pair, :], oT[pair % 2][:, :], o_hi[:, pair, :].bitcast(F32), ALU.subtract).then_inc(o_split, 1)
                    if hp == 1 and cur:
                        normalise(0, 0)
                    if hp == 5 and nxt:
                        normalise(4, 0)
                    if isinstance(b, int) and b == 0:
                        split_wout(hp)

            over_batches(pool, batch)
            phase23_pool(pool)

        @block.scalar
        def _(act):
            need = Need(act)
            act.wait_ge(cond_in, 48)
            nc.scalar.activation(sig[:, :, :], condT_sb[:, :, :], ACT.Tanh, scale=0.5).then_inc(tanh_done, 1)

            def weights_high(g):
                for c in range(DC):
                    act.wait_ge(w_centred, DC * g + c + 1)
                    nc.scalar.activation(split_qk(w_hi, g, c), raw_qk(g, c), ACT.Copy).then_inc(wqk_hi_ready, 1)
                if g == 0:
                    act.wait_ge(wv_in, DC * 16)
                    for c in range(DC):
                        nc.scalar.activation(w_hi[:, c, 2 * H * HD:], raw_v(c), ACT.Copy).then_inc(wv_hi_ready, 1)

            def chunk(b, hp, pos):
                key = (hp, pos)
                bank = ch[slot_bank(b, key)]
                name, t = CHUNKS[key]
                g = group_of(b, hp)
                need(slot_filled, through("slot", b, key))
                if name != "v":
                    c = 2 * t + pos
                    need(qn_ready if c >= POOL_CHUNKS else qn_pool_ready, g)
                    nc.scalar.activation(raw[:, c, :], bank[:, :], ACT.Copy)
                    need(chunk_summed, through("chunk", b, key) - 2)
                    nc.scalar.activation(sq[c % 2][:, :], bank[:, :], ACT.Square).then_inc(act_read, 1)
                else:
                    need(attended, (g - 1) * GU)
                    nc.scalar.activation(V[1 if hp in ODD_STEPS else 0][:, t, :], bank[:, :], ACT.Copy).then_inc(act_read, 1)

            def batch(b, cur, nxt, prv):
                for hp in range(UNITS):
                    u = b * UNITS + hp
                    par = (hp + 1) % 2
                    ahead = (cur and nxt) or (cur and hp < UNITS - 1) or (nxt and hp == UNITS - 1)
                    live = (hp, 0) in CHUNKS and (cur if hp < 2 else nxt)
                    if ahead:
                        need(qk_transposed, u + 2)
                        need(scored, u)
                        if isinstance(b, int) and b < 0:
                            need(pads_ready, 4)
                        nc.scalar.activation(q_hi[par][0:64, 0, :], pq[0:64, 0:N], ACT.Identity,
                                             bias=vec[0:64, BQ:BQ + 1], scale=vec[0:64, GQ:GQ + 1])
                        nc.scalar.activation(q_hi[par][64:128, 1, :], pq[64:128, 0:N], ACT.Identity,
                                             bias=vec[64:128, BQ:BQ + 1], scale=vec[64:128, GQ:GQ + 1])
                        nc.scalar.activation(k_hi[par][:, :], pq[:, N:2 * N], ACT.Identity,
                                             bias=vec[:, BK:BK + 1], scale=vec[:, GK:GK + 1]).then_inc(hi_ready, 1)
                        need(lo_ready, u)
                        nc.scalar.activation(qkT[par][:, 0:N], pq[:, 0:N], ACT.Identity,
                                             bias=vec[:, BQ:BQ + 1], scale=vec[:, GQ:GQ + 1])
                        nc.scalar.activation(qkT[par][:, N:2 * N], pq[:, N:2 * N], ACT.Identity,
                                             bias=vec[:, BK:BK + 1], scale=vec[:, GK:GK + 1]).then_inc(qk_evacuated, 1)
                    if isinstance(b, int) and b < 0 and hp in (2, 5):
                        weights_high(0 if hp == 2 else 1)
                    if live:
                        chunk(b, hp, 0)
                    if hp == 6 and prv:
                        need(slot_filled, through("slot", b, (6, 0)))
                        nc.scalar.activation(tokT[:, :, :].rearrange("p c n -> p (c n)"),
                                             ch[slot_bank(b, (6, 0))][:, :], ACT.Copy).then_inc(act_read, 1)
                    if cur:
                        need(scored, u + 1)
                        need(attended, u - 1)
                        nc.scalar.activation(prob[hp % 2][:, :], sc[:, :], ACT.Exp, scale=HD ** -0.5).then_inc(prob_ready, 1)
                    if live:
                        chunk(b, hp, 1)
                    if hp == 1 and nxt:
                        need(slot_filled, through("slot", b, (1, 2)))
                        need(bias1_ready, 1)
                        need(hT_split, b + 1)
                        bank = ch[slot_bank(b, (1, 2))]
                        for c in range(DC):
                            bias = (bias1[:, c, b + 1:b + 2] if isinstance(b, int) else bias1[:, c, bass.ds(b + 1, 1)])
                            ins = nc.scalar.activation(hT[:, c, :], bank[:, c * N:(c + 1) * N], ACT.Identity,
                                                       bias=bias, scale=vec[:, LN1_G + c:LN1_G + c + 1])
                        ins.then_inc(act_read, 1)

            over_batches(act, batch)
            phase23_scalar(act)

        def rsqrt(chain, n, dst):
            v, y, a = var[:, 0:n], ny[:, 0:n], na[:, 0:n]
            half = var_half[:, 0:n]
            chain(nc.vector.tensor_scalar(half, v.bitcast(I32), 1, None, ALU.logical_shift_right))
            chain(nc.vector.tensor_scalar(y.bitcast(I32), half, -1.0, float(0x5F3759DF), ALU.mult, ALU.add))
            for r in range(NEWTON):
                chain(nc.vector.scalar_tensor_tensor(a, y, -0.5, y, ALU.mult, ALU.mult))
                chain(nc.vector.tensor_tensor(a, a, v, ALU.mult))
                if r < NEWTON - 1:
                    chain(nc.vector.scalar_tensor_tensor(y, a, 1.5, y, ALU.add, ALU.mult))
                else:
                    nc.vector.scalar_tensor_tensor(dst[:, 0:n], a, 1.5, y, ALU.add, ALU.mult).then_inc(rstd_ready, 1)

        @block.vector
        def _(dve):
            need = Need(dve)
            chain = Chain(dve, dve_step)
            nc.vector.memset(mv[:, :, :], 1.0)
            chain(nc.vector.memset(var[:, :], 1.0))

            def silu_of_condition():
                dve.wait_ge(tanh_done, 1)
                chain(nc.vector.scalar_tensor_tensor(sig[:, :, :], sig[:, :, :], 1.0, condT_sb[:, :, :], ALU.add, ALU.mult))
                nc.vector.tensor_scalar(silu[:, :, :], sig[:, :, :], 0.5, None, ALU.mult).then_inc(silu_ready, 1)
                dve.wait_ge(con_in, 16)
                nc.vector.tensor_scalar(neg_ident[:, :], ident, -1.0, None, ALU.mult).then_inc(consts_ready, 1)
                nc.vector.tensor_copy(same_b[:, :], same_expert).then_inc(consts_ready, 1)

            def shift():
                dve.wait_ge(shift_done, 1)
                for c in range(DC):
                    ins = nc.vector.tensor_scalar(bias1[:, c, :], av[:, c * B:(c + 1) * B], vec[:, B_ADA + c:B_ADA + c + 1],
                                                  vec[:, LN1_B + c:LN1_B + c + 1], ALU.add, ALU.add)
                ins.then_inc(bias1_ready, 1)

            def centre(g, c):
                w4 = raw_qk(g, c).rearrange("p a (h d) -> p (a h) d", d=HD)
                means = w_means[:, 2 * g + c, :]
                dve.wait_ge(wqk_in[g][c], 16)
                chain(nc.vector.tensor_reduce(means, w4, AX.X, ALU.add))
                chain(nc.vector.tensor_scalar(means, means, 1.0 / HD, None, ALU.mult))
                nc.vector.tensor_tensor(w4, w4, means.rearrange("p (h o) -> p h o", o=1).to_broadcast([P, 2 * GU * 2, HD]),
                                        ALU.subtract).then_inc(w_centred, 1)

            def first_low_parts():
                for c in range(DC):
                    dve.wait_ge(wqk_hi_ready, c + 1)
                    nc.vector.tensor_tensor(split_qk(w_lo, 0, c), raw_qk(0, c), split_qk(w_hi, 0, c).bitcast(F32),
                                            ALU.subtract).then_inc(w_lo_first_ready, 1)

            def row_stats(rows, at):
                for t in range(TT):
                    ins = nc.vector.bn_stats(bn[:, at + t, :], rows[:, t, :])
                ins.then_inc(dve_step, 1)
                chain.n += 1
                dve.wait_ge(dve_step, chain.count())
                nc.vector.memset(held_v[:, :], 0.0)
                for t in range(TT):
                    ins = nc.vector.bn_aggr(mv[:, at + t, :], bn[:, at + t, :])
                chain(ins)

            def token_rows(b):
                need(rstd_ready, through("newton", b, 4))
                need(row_out, (b - 1) * 16)
                for t in range(TT):
                    ins = nc.vector.tensor_scalar(xh2[:, t, :], tok[:, t, :], mv[:, 2 + t, 0:1],
                                                  rstd[0][:, NH + 2 + t:NH + 3 + t], ALU.subtract, ALU.mult)
                ins.then_inc(xh2_ready, 1)

            def last_rows():
                row_stats(tok, 2)
                chain(nc.vector.tensor_scalar(var[:, NH + 2:NH + 4], mv[:, 2:4, 1], EPS, None, ALU.add))
                rsqrt(chain, NH + 4, rstd[0])
                token_rows(B)

            def head_sums(b, hp, pos):
                name, t = CHUNKS[hp, pos]
                c = 2 * t + pos
                need(act_read, through("act", b, (hp, pos)))
                nc.vector.tensor_reduce(ssum[:, c * 8:(c + 1) * 8],
                                        sq[c % 2][:, :].rearrange("p (h d) -> p h d", d=HD), AX.X, ALU.add).then_inc(chunk_summed, 1)

            def batch(b, cur, nxt, prv):
                last_entry = isinstance(b, int) and b == B
                for hp in range(UNITS):
                    u = b * UNITS + hp
                    if hp == 1 and prv:
                        need(slot_filled, through("slot", b, (0, 2)))
                        need(xr_in, b * 16)
                        need(tok_out, (b - 1) * 16)
                        need(xh2_ready, b - 1)
                        nc.vector.tensor_tensor(tok[:, :, :].rearrange("p t d -> p (t d)"), ch[slot_bank(b, (0, 2))][:, :],
                                                xr_sb[:, :, :].rearrange("p t d -> p (t d)"), ALU.add).then_inc(dve_read, 1)
                    if isinstance(b, int) and b < 0 and hp == 2:
                        silu_of_condition()
                        centre(0, 0)
                        shift()
                        centre(0, 1)
                    if hp == 2 and nxt:
                        need(act_read, through("act", b, (1, 2)))
                        chain(nc.vector.tensor_copy(hT_hi[:, :, :], hT[:, :, :]))
                        nc.vector.tensor_tensor(hT_lo[:, :, :], hT[:, :, :], hT_hi[:, :, :].bitcast(F32), ALU.subtract).then_inc(hT_split, 1)
                    if isinstance(b, int) and b < 0 and hp == 2:
                        first_low_parts()
                    if isinstance(b, int) and b < 0 and hp in (3, 4):
                        centre(1, hp - 3)
                    if hp == 1 and nxt:
                        need(rstd_ready, through("newton", b, 0))
                        if cur:
                            need(slot_filled, through("slot", b - 1, (1, 2)))
                        for t in range(TT):
                            ins = nc.vector.tensor_scalar(xh[:, t, :], x_sb[:, t, :], mv[:, t, 0:1],
                                                          rstd[1][:, NH + t:NH + t + 1], ALU.subtract, ALU.mult)
                        ins.then_inc(xh_ready, 1)
                    if (cur and hp > 0) or (hp == 0 and prv):
                        need(attended, u)
                        need(divided, u - 1)
                        need(o_split, u - 2)
                        chain(nc.vector.reciprocal(rec[:, :], av[:, N:2 * N]))
                        o = oT[(hp - 1) % 2]
                        nc.vector.tensor_tensor(o[:, :], av[:, 0:N], rec[:, :], ALU.mult).then_inc(divided, 1)
                        need(divided, u)
                        if hp == 1 and prv:
                            need(slot_filled, through("slot", b, (0, 2)))
                        nc.vector.tensor_copy(o_hi[:, (hp - 1) % UNITS, :], o[:, :]).then_inc(normed, 1)
                    if hp == 0 and nxt:
                        need(x_in, (b + 2) * 16)
                        row_stats(x_sb, 0)
                    if hp in (0, 3, 4, 7) and (cur if hp < 2 else nxt):
                        head_sums(b, hp, 0)
                        head_sums(b, hp, 1)
                    if hp == 6 and prv:
                        need(slot_filled, through("slot", b, (6, 1)))
                        dst = (logit[:, (b - 1) * TT:b * TT, :].rearrange("p t e -> p (t e)") if isinstance(b, int)
                               else logit[:, :, :].rearrange("p t e -> p (t e)")[:, bass.ds((b - 1) * TT * E, TT * E)])
                        nc.vector.tensor_copy(dst, ch[slot_bank(b, (6, 1))][:, 0:TT * E]).then_inc(dve_read, 1)
                    if (cur and nxt) or (cur and hp < UNITS - 1) or (nxt and hp == UNITS - 1):
                        need(pre_scored, u + 2)
                        need(scored, u)
                        nc.vector.tensor_reduce(m[(hp + 1) % 2][:, :], mx[:, :].rearrange("p (a j) -> p a j", a=4),
                                                AX.X, ALU.max).then_inc(max_ready, 1)
                    if hp == 5 and prv and not last_entry:
                        token_rows(b)
                    if (hp == 1 and cur) or (hp == 5 and nxt):
                        g = b * 2 + (1 if hp == 1 else 2)
                        need(rstd_ready, through("newton", b, hp - 1))
                        need(qk_transposed, (g - 1) * GU)
                        for c in range(POOL_CHUNKS, 4):
                            ins = times_rstd(nc.vector, 1 if hp == 1 else 0, c)
                        ins.then_inc(qn_ready, 1)
                    if hp == 2 and prv and not last_entry:
                        need(dve_read, through("dve", b, (0, 2)))
                        row_stats(tok, 2)
                    if (hp == 0 and (cur or nxt)) or (hp == 4 and (nxt or prv) and not last_entry):
                        if cur if hp == 0 else nxt:
                            need(chunk_summed, through("chunk", b, (hp, 1)))
                            chain(nc.vector.tensor_scalar(var[:, 0:NH], ssum[:, :], 1.0 / HD, EPS, ALU.mult, ALU.add))
                        at = 0 if hp == 0 else 2
                        chain(nc.vector.tensor_scalar(var[:, NH + at:NH + at + 2], mv[:, at:at + 2, 1], EPS, None, ALU.add))
                        if hp == 0 and cur:
                            need(qn_pool_ready, b * 2)
                        if hp == 4 and (cur or nxt):
                            need(qn_pool_ready, b * 2 + 1)
                        rsqrt(chain, NH + at + 2, rstd[1 if hp == 0 else 0])


            per = 37
            def counted(b, cur, nxt, prv):
                before = chain.n
                if not isinstance(b, int):
                    chain.base = (b - FIRST_LOOPED) * per
                batch(b, cur, nxt, prv)
                if not isinstance(b, int):
                    assert chain.n - before == per, chain.n - before
                    chain.base = per * (LAST_LOOPED - FIRST_LOOPED)
            over_batches(dve, counted)
            phase23_vector(dve, chain, last_rows)

        @block.tensor
        def _(pe):
            need = Need(pe)
            pe.wait_ge(cond_in, 48)
            pe.wait_ge(silu_ready, 1)
            for mc in range(DC):
                for c in range(DC):
                    ins = nc.tensor.matmul(av[:, mc * B:(mc + 1) * B], wada_sb[:, c, mc * P:(mc + 1) * P], silu[:, c, :],
                                           start=(c == 0), stop=(c == DC - 1))
            ins.then_inc(shift_done, 1)
            pe.wait_ge(consts_ready, 2)

            def take_bank(b, key):
                free = bank_free(b, key)
                if free:
                    need(free_sem[free[0]], free[1])
                return ch[slot_bank(b, key)]

            def chunk(b, hp, pos):
                bank = take_bank(b, (hp, pos))
                name, t = CHUNKS[hp, pos]
                if pos == 0:
                    need(hT_split, b + 1 if hp < 2 else b + 2)
                if isinstance(b, int) and b < 0 and pos == 0:
                    if hp == 3:
                        need(w_lo_first_ready, DC)
                    if hp == 5:
                        need(w_lo_rest_ready, DC)
                    if hp == 7:
                        need(w_lo_rest_ready, 2 * DC)
                col = "qkv".index(name) * H * HD + (GW if hp in ODD_STEPS else 0)
                for c in range(DC):
                    ins = three_passes(bank[:, :], hT_hi[:, c, t * P:(t + 1) * P], hT_lo[:, c, t * P:(t + 1) * P],
                                       w_hi[:, c, col:col + GW], w_lo[:, c, col:col + GW], c == 0, c == DC - 1)
                ins.then_inc(slot_filled, 1)

            def transposed(bank, rows):
                for c in range(DC):
                    for t in range(TT):
                        ins = nc.tensor.transpose(bank[:, c * N + t * P:c * N + (t + 1) * P], rows[:, t, c * P:(c + 1) * P], ident)
                ins.then_inc(slot_filled, 1)

            def batch(b, cur, nxt, prv):
                for hp in range(UNITS):
                    u = b * UNITS + hp
                    ahead = (cur and nxt) or (cur and hp < UNITS - 1) or (nxt and hp == UNITS - 1)
                    npar = (hp + 1) % 2
                    live = (hp, 0) in CHUNKS and (cur if hp < 2 else nxt)
                    if ahead:
                        gpar, i = ((hp + 1) // GU) % 2, (hp + 1) % GU
                        need(qn_ready, b * 2 + (hp + 1) // GU + 1)
                        need(qn_pool_ready, b * 2 + (hp + 1) // GU + 1)
                        need(qk_evacuated, u + 1)
                        for c, at in ((0, 0), (2, 1), (1, 2), (3, 3)):
                            ins = nc.tensor.transpose(pq[:, at * P:(at + 1) * P], qn[gpar][:, c, i * P:(i + 1) * P], ident)
                        ins.then_inc(qk_transposed, 1)
                    if live:
                        chunk(b, hp, 0)
                    if hp == 6 and prv:
                        bank = take_bank(b, (6, 0))
                        need(dve_read, through("dve", b, (0, 2)))
                        transposed(bank, tok)
                    if (cur and hp > 0) or (hp == 0 and prv):
                        need(prob_ready, u)
                        need(divided, u - 1)
                        i = (hp - 1) % GU
                        gpar = ((hp - 1) // GU) % 2
                        if i == 0:
                            need(act_read, through("act", b, (1, 1)) if hp == 5 else through("act", b, (0, 0)) - 1)
                            if isinstance(b, int) and b == 0:
                                need(pads_ready, 5)
                        for jt in range(TT):
                            for hh in range(2):
                                at = hh * TT * N + jt * N
                                nc.tensor.matmul(av[hh * HD:(hh + 1) * HD, 0:N], V[gpar][:, jt, i * P + hh * HD:i * P + (hh + 1) * HD],
                                                 prob[(hp - 1) % 2][:, at:at + N], start=(jt == 0), stop=(jt == TT - 1))
                        need(prob_summed, u)
                        for hh in range(2):
                            ins = nc.tensor.matmul(av[hh * HD:(hh + 1) * HD, N:2 * N], ones[:, :], prob_sum[(hp - 1) % 2][:, hh, :],
                                                   start=True, stop=True)
                        ins.then_inc(attended, 1)
                    if cur:
                        need(prob_ready, u)
                        need(max_ready, u + 1)
                        need(lo_ready, u + 1)
                        par = hp % 2
                        for hh in range(2):
                            for jt in range(TT):
                                at = hh * TT * N + jt * N
                                keys = slice(jt * P, (jt + 1) * P)
                                three_passes(sc[:, at:at + N], k_hi[par][:, keys], k_lo[par][:, keys],
                                             q_hi[par][:, hh, :], q_lo[par][:, hh, :], True, False)
                                for it in range(TT):
                                    ins = nc.tensor.matmul(sc[:, at + it * P:at + (it + 1) * P],
                                                           m[par][:, it * 2 + hh:it * 2 + hh + 1].to_broadcast([P, P]),
                                                           neg_ident[:, :], start=False, stop=(it == TT - 1))
                        ins.then_inc(scored, 1)
                    if live:
                        chunk(b, hp, 1)
                    if hp == 1 and nxt:
                        bank = take_bank(b, (1, 2))
                        need(xh_ready, b + 2)
                        transposed(bank, xh)
                    if hp == 6 and prv:
                        bank = take_bank(b, (6, 1))
                        need(act_read, through("act", b, (6, 0)))
                        for t in range(TT):
                            for c in range(DC):
                                ins = nc.tensor.matmul(bank[:, t * E:(t + 1) * E], tokT[:, c, t * P:(t + 1) * P], wg_sb[:, c, :],
                                                       start=(c == 0), stop=(c == DC - 1))
                        ins.then_inc(slot_filled, 1)
                    if ahead:
                        need(hi_ready, u + 2)
                        need(max_ready, u + 1)
                        for it in range(TT):
                            for hh in range(2):
                                at = (it * 2 + hh) * N
                                ins = nc.tensor.matmul(mx[:, at:at + N], q_hi[npar][:, hh, it * P:(it + 1) * P], k_hi[npar][:, :],
                                                       start=True, stop=True)
                        ins.then_inc(pre_scored, 1)
                    if hp == 0 and prv:
                        bank = take_bank(b, (0, 2))
                        need(o_split, u - 1)
                        if isinstance(b, int) and b == 1:
                            need(wo_ready, 2 * UNITS)
                        for t in range(TT):
                            for pair in range(UNITS):
                                if t == 0 and pair == UNITS - 1:
                                    need(o_split, u)
                                ins = three_passes(bank[:, t * D:(t + 1) * D], o_hi[:, pair, t * P:(t + 1) * P], o_lo[:, pair, t * P:(t + 1) * P],
                                                   wo_hi[:, pair, :], wo_lo[:, pair, :], pair == 0, pair == UNITS - 1)
                        ins.then_inc(slot_filled, 1)

            over_batches(pe, batch)
            phase23_tensor(pe)


def kernel(**inputs):
    import concourse.bacc as bacc
    from concourse.bass_utils import run_bass_kernel_spmd

    a = {k.removeprefix("L0_cond_"): np.asarray(v) for k, v in inputs.items()}

    def by_partition(w):
        return np.ascontiguousarray(w.reshape(-1, P, w.shape[-1]).transpose(1, 0, 2))

    def columns(v):
        return v.reshape(-1, P).T

    twice = lambda v: np.concatenate([v, v])[:, None]
    vecs = np.concatenate([columns(a["ln1_g"]), columns(a["ln1_b"]), columns(a["b_ada"]), columns(a["mlp_g"]), columns(a["mlp_b"]),
                           twice(a["qn_g"]), twice(a["qn_b"]), twice(a["kn_g"]), twice(a["kn_b"])], axis=1)
    fc1 = a["fc1s"].transpose(0, 2, 1).reshape(E, DC, P, DD).transpose(0, 2, 1, 3).reshape(E, P, DC * DD)
    fc2 = a["fc2s"].transpose(0, 2, 1).reshape(E, HC, P, D).transpose(0, 2, 1, 3).reshape(E, P, HC * D)
    b1 = a["b1s"].reshape(E, HC, P).transpose(0, 2, 1)
    p = np.arange(P)
    same = (p[:, None] % E == p[None, :] % E)
    consts = np.concatenate([np.eye(P), same, same & (p[:, None] < p[None, :]),
                             np.broadcast_to(np.arange(32), (P, 32)), p[:, None],
                             p[:, None] % 8 == np.arange(8), p[:, None] // 8 == np.arange(4 * KT)], axis=1).astype(np.float32)
    arrays = {
        "x": a["x"],
        "condT": by_partition(a["cond_1024"].T),
        "w_adaT": by_partition(a["W_ada"].T),
        "vecs": np.ascontiguousarray(vecs),
        "w_qkvT": by_partition(a["Wqkv"].T),
        "w_outT": by_partition(a["Wout"].T),
        "w_gateT": by_partition(a["Wgate"].T),
        "experts": np.ascontiguousarray(np.concatenate([fc1, fc2, b1], axis=2)),
        "b2s": a["b2s"],
        "consts": consts,
    }
    nc = bacc.Bacc("TRN2", target_bir_lowering=False, num_devices=1)
    aps = [nc.dram_tensor(k, v.shape, F32, kind="ExternalInput").ap() for k, v in arrays.items()]
    out = nc.dram_tensor("out", (B, N, D), F32, kind="ExternalOutput").ap()
    build(nc, *aps, out)
    r = run_bass_kernel_spmd(nc, [arrays], core_ids=[0])
    return r.results[0]["out"]
```
